# Optimizing a Trainium2 kernel written in Bass

```python
import numpy as np
import jax
import jax.numpy as jnp

def _softmax(x, axis=-1):
    return jax.nn.softmax(x, axis=axis)

def _gelu(x):
    return jax.nn.gelu(x, approximate=True)

def _silu(x):
    return jax.nn.silu(x)

def _sigmoid(x):
    return jax.nn.sigmoid(x)

def _layernorm(x, axis=-1, eps=1e-05):
    m = jnp.mean(x, axis=axis, keepdims=True)
    v = jnp.var(x, axis=axis, keepdims=True)
    return (x - m) / jnp.sqrt(v + eps)

def _scatter_add(tgt, idx, src, axis=0):
    return tgt.at[idx].add(src)

def _segment_sum(src, seg, n):
    return jax.ops.segment_sum(src, seg, n)
kernel_name = 'mk_macaron_d1_jaxref_r8_85c9bf'

def setup_inputs(seed: int=0):
    np.random.seed(seed)
    _w = jnp.asarray

    def _L0_attn_setup():
        import jax, jax.numpy as jnp
        import numpy as np
        N_HEAD = 16
        D_K = 64
        D_V = 64
        EMBED = 128
        BATCH = 4
        SEQ = 256
        key = jax.random.key(seed)
        ks = jax.random.split(key, 12)
        s = lambda d: 1.0 / np.sqrt(d)
        u = lambda k, shape, d: jax.random.uniform(k, shape, jnp.float32, -s(d), s(d))
        return {'z': jax.random.normal(ks[0], (BATCH, SEQ, EMBED), jnp.float32), 'wq': u(ks[1], (EMBED, D_K), D_K), 'wk': u(ks[2], (EMBED, D_K), D_K), 'wv': u(ks[3], (EMBED, D_V), D_V), 'fcq_w': u(ks[4], (D_K, N_HEAD * D_K), D_K), 'fcq_b': u(ks[5], (N_HEAD * D_K,), N_HEAD * D_K), 'fck_w': u(ks[6], (D_K, N_HEAD * D_K), D_K), 'fck_b': u(ks[7], (N_HEAD * D_K,), N_HEAD * D_K), 'fcv_w': u(ks[8], (D_V, N_HEAD * D_V), D_V), 'fcv_b': u(ks[9], (N_HEAD * D_V,), N_HEAD * D_V), 'fco_w': u(ks[10], (N_HEAD * D_V, EMBED), EMBED), 'fco_b': u(ks[11], (EMBED,), EMBED)}
    _L0_attn_in = _L0_attn_setup()

    def _L0_ffn_setup():
        import jax, jax.numpy as jnp
        import numpy as np
        B, S, D, E, F, TOP_K = (4, 256, 128, 8, 512, 2)
        key = jax.random.key(seed)
        k0, k1, k2, k3 = jax.random.split(key, 4)
        init = lambda k, shape, fan: (jax.random.normal(k, shape, jnp.float32) / np.sqrt(fan)).astype(jnp.float32)
        return {'x': jax.random.normal(k0, (B, S, D), jnp.float32), 'gate_w': init(k1, (D, E), D), 'w1': init(k2, (E, D, F), D), 'b1': jnp.zeros((E, F), jnp.float32), 'w2': init(k3, (E, F, D), F), 'b2': jnp.zeros((E, D), jnp.float32)}
    _L0_ffn_in = _L0_ffn_setup()
    _d = {'L0_attn_z': _L0_attn_in['z'], 'L0_attn_wq': _L0_attn_in['wq'], 'L0_attn_wk': _L0_attn_in['wk'], 'L0_attn_wv': _L0_attn_in['wv'], 'L0_attn_fcq_w': _L0_attn_in['fcq_w'], 'L0_attn_fcq_b': _L0_attn_in['fcq_b'], 'L0_attn_fck_w': _L0_attn_in['fck_w'], 'L0_attn_fck_b': _L0_attn_in['fck_b'], 'L0_attn_fcv_w': _L0_attn_in['fcv_w'], 'L0_attn_fcv_b': _L0_attn_in['fcv_b'], 'L0_attn_fco_w': _L0_attn_in['fco_w'], 'L0_attn_fco_b': _L0_attn_in['fco_b'], 'L0_ffn_gate_w': _L0_ffn_in['gate_w'], 'L0_ffn_w1': _L0_ffn_in['w1'], 'L0_ffn_b1': _L0_ffn_in['b1'], 'L0_ffn_w2': _L0_ffn_in['w2'], 'L0_ffn_b2': _L0_ffn_in['b2']}
    _x0 = _d['L0_attn_z']
    _d['L0_attn_z'] = jax.random.normal(jax.random.fold_in(jax.random.key(seed), 1), (2, 1024, 128), dtype=_x0.dtype)
    del _x0
    return _d

def reference(L0_attn_z, L0_attn_wq, L0_attn_wk, L0_attn_wv, L0_attn_fcq_w, L0_attn_fcq_b, L0_attn_fck_w, L0_attn_fck_b, L0_attn_fcv_w, L0_attn_fcv_b, L0_attn_fco_w, L0_attn_fco_b, L0_ffn_gate_w, L0_ffn_w1, L0_ffn_b1, L0_ffn_w2, L0_ffn_b2):

    def _L0_attn_ref(z, wq, wk, wv, fcq_w, fcq_b, fck_w, fck_b, fcv_w, fcv_b, fco_w, fco_b):
        import jax, jax.numpy as jnp
        import numpy as np
        N_HEAD = 16
        D_K = 64
        D_V = 64
        EMBED = 128
        BATCH = 4
        SEQ = 256
        b, n, _ = z.shape
        scale = jnp.sqrt(jnp.float32(D_K))
        q = z @ wq @ fcq_w + fcq_b
        k = z @ wk @ fck_w + fck_b
        v = z @ wv @ fcv_w + fcv_b
        q = q.reshape(b, n, N_HEAD, D_K)
        k = k.reshape(b, n, N_HEAD, D_K)
        v = v.reshape(b, n, N_HEAD, D_V)
        scores = jnp.einsum('bihd,bjhd->bhij', q, k) / scale
        attn = jax.nn.softmax(scores, axis=-1)
        out = jnp.einsum('bhij,bjhd->bihd', attn, v)
        out = out.reshape(b, n, N_HEAD * D_V)
        return out @ fco_w + fco_b

    def _L0_ffn_ref(x, gate_w, w1, b1, w2, b2):
        import jax, jax.numpy as jnp
        import numpy as np
        B, S, D, E, F, TOP_K = (4, 256, 128, 8, 512, 2)
        b, s, d = x.shape
        e = gate_w.shape[1]
        xf = x.reshape(-1, d)
        t = xf.shape[0]
        logits = xf @ gate_w
        top_w, top_idx = jax.lax.top_k(logits, TOP_K)
        top_w = jax.nn.softmax(top_w.astype(jnp.float32), axis=-1).astype(x.dtype)
        combine = jnp.zeros((t, e), x.dtype).at[jnp.arange(t)[:, None], top_idx].add(top_w)
        h = jax.nn.gelu(jnp.einsum('td,edf->tef', xf, w1) + b1, approximate=False)
        y = jnp.einsum('tef,efd->ted', h, w2) + b2
        out = jnp.einsum('ted,te->td', y, combine)
        return out.reshape(b, s, d)
    x = L0_attn_z
    x = x + 0.5 * _L0_ffn_ref(_layernorm(x, axis=-1), L0_ffn_gate_w, L0_ffn_w1, L0_ffn_b1, L0_ffn_w2, L0_ffn_b2)
    x = x + _L0_attn_ref(_layernorm(x, axis=-1), L0_attn_wq, L0_attn_wk, L0_attn_wv, L0_attn_fcq_w, L0_attn_fcq_b, L0_attn_fck_w, L0_attn_fck_b, L0_attn_fcv_w, L0_attn_fcv_b, L0_attn_fco_w, L0_attn_fco_b)
    x = x + 0.5 * _L0_ffn_ref(_layernorm(x, axis=-1), L0_ffn_gate_w, L0_ffn_w1, L0_ffn_b1, L0_ffn_w2, L0_ffn_b2)
    return x

_drawn_inputs = setup_inputs


def setup_inputs(seed=0):
    import zlib

    import numpy as np

    out = dict(_drawn_inputs(seed))
    spreads = {'L0_ffn_b1': (0.0, 0.1), 'L0_ffn_b2': (0.0, 0.1)}
    factors = {'L0_attn_wq': 2.694, 'L0_attn_fcq_b': 40.32, 'L0_attn_fck_b': 64.0}
    for name, (base, spread) in spreads.items():
        noise = np.random.default_rng([zlib.crc32(name.encode()), seed]).standard_normal(out[name].shape)
        drawn = base * np.exp(spread * noise) if base else spread * noise
        out[name] = jnp.asarray(drawn.astype(out[name].dtype))
    for name, factor in factors.items():
        out[name] = (out[name] * factor).astype(out[name].dtype)
    return out
```

```python
from contextlib import ExitStack

import concourse.bass as bass
from concourse import mybir

F32 = mybir.dt.float32
F16 = mybir.dt.float16
BF16 = mybir.dt.bfloat16
ACT = mybir.ActivationFunctionType
ALU = mybir.AluOpType
AX = mybir.AxisListType
ds = bass.ds


def macaron_block(nc, z, wq, wk, wv, fcq_w, fcq_b, fck_w, fck_b, fcv_w, fcv_b, fco_w, fco_b,
                  gate_w, w1, b1, w2, b2, out):
    P = 128
    BATCH, SEQ, D = z.shape
    T = BATCH * SEQ
    NT = T // P
    TGW = 512
    TG = T // TGW
    TPG = TGW // P
    E, _, F = w1.shape
    FB = F // P
    DK = wq.shape[1]
    H = fcq_w.shape[1] // DK
    NH = BATCH * H
    JB = SEQ // P
    HALVES = SEQ // TGW
    STEPS = JB * HALVES
    VW = 2 * DK + 1
    PAIRS = H * DK // P
    UNITS = TG * E
    EPS = 1e-5
    SCALE = float(DK) ** -0.5
    assert (D, DK, F, JB, STEPS) == (128, 64, 512, 8, 16)

    z_t = z.rearrange("b (n p) d -> p (b n) d", p=P)
    out_t = out.rearrange("b (n p) d -> p (b n) d", p=P)

    with ExitStack() as ctx:
        def sb(name, shape, dt):
            return ctx.enter_context(nc.sbuf_tensor(name, shape, dt))

        def sem(name):
            return ctx.enter_context(nc.semaphore(name))

        bank = [ctx.enter_context(nc.psum_tensor(f"bank{i}", [P, 512], F32))[:, :] for i in range(6)]
        duo = ctx.enter_context(nc.psum_tensor("duo", [P, 2, 512], F32))
        bank += [duo[:, 0, :], duo[:, 1, :]]

        x = sb("x", [P, NT * D], F32)
        xh = sb("xh", [P, T], F16)
        xl = sb("xl", [P, T], F16)
        w1h = sb("w1h", [P, E * F], F16)
        w1l = sb("w1l", [P, E * F], F16)
        w2h = sb("w2h", [P, E * FB * D], F16)
        w2l = sb("w2l", [P, E * FB * D], F16)
        b1c = sb("b1c", [P, E * FB], F32)
        b2diag = sb("b2diag", [P, NT * D], F32)
        gh = sb("gh", [P, E], F16)
        gl = sb("gl", [P, E], F16)
        gate32 = sb("gate32", [P, E], F32)
        ident = sb("ident", [P, P], F32)
        ident16 = sb("ident16", [P, P], F16)
        before = sb("before", [P, E, E], F32)
        qkbias = sb("qkbias", [P, H, 2], F32)
        hbias = [sb(f"hbias{i}", [P, 2], F32) for i in range(2)]
        vbias = sb("vbias", [P, H * DK], F32)
        obias = sb("obias", [P, D], F32)
        pw32 = sb("pw32", [P, 3, DK], F32)
        pwh = sb("pwh", [P, 3, 2, DK], F16)
        pwl = sb("pwl", [P, 3, 2, DK], F16)
        fqk_h = sb("fqk_h", [P, 2, H, 2, DK], F16)
        fqk_l = sb("fqk_l", [P, 2, H, 2, DK], F16)
        fv_h = sb("fv_h", [P, H * DK], F16)
        fv_l = sb("fv_l", [P, H * DK], F16)
        fo_h = sb("fo_h", [P, PAIRS * D], F16)
        fo_l = sb("fo_l", [P, PAIRS * D], F16)
        u = [sb(f"u{n}", [P, T], F16) for n in "qkv"]

        stats = sb("stats", [P, NT, 6], F32)
        mv = sb("mv", [P, NT, 2], F32)
        var_eps = sb("var_eps", [P, NT], F32)
        sd = sb("sd", [P, NT], F32)
        rstd = sb("rstd", [P, NT], F32)
        logit = sb("logit", [P, NT, E], F32)
        rank = sb("rank", [P, NT, E], F32)
        sel = sb("sel", [P, 2, NT, E], F32)
        picked = sb("picked", [P, NT, E], F32)
        top = sb("top", [P, 2, NT], F32)
        gap = sb("gap", [P, NT], F32)
        expgap = sb("expgap", [P, NT], F32)
        wtop = sb("wtop", [P, 3, NT], F32)
        comb = sb("comb", [P, NT, E], F32)
        combT = sb("combT", [P, P], F32)

        heads = sb("heads", [P, NT, H * DK], F32)
        stage = heads[:, :, :].rearrange("p n d -> p (n d)")
        w1_32 = stage[:, 0:E * F]
        w2_32 = stage[:, E * F:2 * E * F]
        fqk_32 = stage[:, 2 * E * F:2 * E * F + 2 * H * DK].rearrange("p (w h d) -> p w h d", w=2, h=H)
        fv_32 = stage[:, 2 * E * F + 2 * H * DK:2 * E * F + 3 * H * DK]
        fo_32 = stage[:, 2 * E * F + 3 * H * DK:2 * E * F + 4 * H * DK]

        work = sb("work", [P, 8256], F32)

        def view(a, n, dt=F32):
            v = work[:, a:a + n]
            return v if dt == F32 else v.bitcast(dt)

        g32 = [[view((2 * q + 0) * 1024 + 512 * f if f < 2 else (2 * q + 1) * 1024 + 512 * (f - 2), 512)
                for f in range(FB)] for q in range(2)]
        hh = [[view(4096 + 1024 * q + 256 * f, 256, F16) for f in range(FB)] for q in range(2)]
        hl = [[view(6144 + 1024 * q + 256 * f, 256, F16) for f in range(FB)] for q in range(2)]

        xn = view(6144, NT * D)
        rows = work[0:E * FB, 0:P]
        qkrows = work[0:H, P:3 * P].rearrange("p (w c) -> p w c", w=2)

        q1 = [view(2048 * i, 512, F16) for i in range(2)]
        q2 = [view(2048 * i + 512, 512, F16) for i in range(2)]
        k1 = [view(2048 * i + 1024, 512, F16) for i in range(2)]
        k2 = [view(2048 * i + 1536, 512, F16) for i in range(2)]
        VPITCH = 132
        vv = [view(4096 + i * JB * VPITCH // 2, JB * VPITCH // 2, F16)
              .rearrange("p (j c) -> p j c", j=JB) for i in range(2)]
        prob = [view(5184 + 512 * i, 512) for i in range(4)]
        plow = [view(7232 + 256 * i, 256, F16) for i in range(4)]
        vsum = sb("vsum", [P, JB, DK], F32)
        acc_sb = sb("acc_sb", [P, JB, VW], F32)
        rsum = sb("rsum", [P, JB], F32)
        tilemax = [sb(f"tilemax{i}", [P, STEPS], F32) for i in range(2)]
        negmax = [sb(f"negmax{i}", [P, JB], F16) for i in range(2)]
        oh = [view(1024 * i, 512, F16) for i in range(2)]
        ol = [view(1024 * i + 512, 512, F16) for i in range(2)]

        x_in = [sem(f"x_in{i}") for i in range(TG)]
        w1_in = [sem(f"w1_in{i}") for i in range(4)]
        w2_in = [sem(f"w2_in{i}") for i in range(4)]
        gate_in, rows_in, b2_in, attn_in, obias_in = (sem(n) for n in ("gate_in", "rows_in", "b2_in", "attn_in", "obias_in"))
        ident_ready, before_ready, b2_zeroed, pad_ready = (sem(n) for n in ("ident_ready", "before_ready", "b2_zeroed", "pad_ready"))
        w1h_ready, w1l_ready, w2h_ready, w2l_ready = (sem(n) for n in ("w1h_ready", "w1l_ready", "w2h_ready", "w2l_ready"))
        gh_ready, gl_ready, ah_ready, al_ready = (sem(n) for n in ("gh_ready", "gl_ready", "ah_ready", "al_ready"))
        bias_turned, bias_ready = sem("bias_turned"), sem("bias_ready")
        var_ready, sd_ready, xn_ready, xn_turned, xh_ready, xl_ready = (
            sem(n) for n in ("var_ready", "sd_ready", "xn_ready", "xn_turned", "xh_ready", "xl_ready"))
        logit_done, gap_ready, expgap_ready, comb_ready, comb_turned, combT_ready, b2_done, b2_added = (
            sem(n) for n in ("logit_done", "gap_ready", "expgap_ready", "comb_ready", "comb_turned", "combT_ready", "b2_done", "b2_added"))
        hid_done, gelu_done, hh_done, hl_done, y_done, y_added = (
            sem(n) for n in ("hid_done", "gelu_done", "hh_done", "hl_done", "y_done", "y_added"))
        u_done, uh_ready, ul_ready = (sem(n) for n in ("u_done", "uh_ready", "ul_ready"))
        qk_done, qk_hi, qk_lo, q2_hi, v_done, v_ready32, v_hi, v_lo = (
            sem(n) for n in ("qk_done", "qk_hi", "qk_lo", "q2_hi", "v_done", "v_ready32", "v_hi", "v_lo"))
        smax_done, smax_red, negmax_ready, mrow_done, mrow_ready = (
            sem(n) for n in ("smax_done", "smax_red", "negmax_ready", "mrow_done", "mrow_ready"))
        st_done, exp_done, plow_pool, plow_dve, pv_done, acc_out, head_ready = (
            sem(n) for n in ("st_done", "exp_done", "plow_pool", "plow_dve", "pv_done", "acc_out", "head_ready"))
        o_turned, oh_ready, ol_ready, o_done, o_added, xbias_added = (
            sem(n) for n in ("o_turned", "oh_ready", "ol_ready", "o_done", "o_added", "xbias_added"))
        norm_step, hbias_ready = sem("norm_step"), sem("hbias_ready")
        dve_step, pool_step, stored = sem("dve_step"), sem("pool_step"), sem("stored")

        def wait(eng, s, v):
            if not (isinstance(v, int) and v <= 0):
                eng.wait_ge(s, v)

        FILLS = [("q", 0), ("k", 0), ("q", 1), ("k", 1), ("v", 0)]
        FILLS += [("m", i) for i in range(STEPS)] + [("r", 0), ("r", 1)]
        AT = [0, 1, 1, 2, 2] + [3, 4, 5, 5, 6, 6, 7, 7, 8, 8, 9, 9, 10, 10, 11, 12] + [14, 14]
        fills_at = [[i for i, a in enumerate(AT) if a == s] for s in range(STEPS)]
        PV_AT = [[(-1, STEPS - 2), (-1, STEPS - 1)], [], [], [(0, 0), (0, 1)]]
        PV_AT += [[(0, s - 2)] for s in range(4, STEPS)]
        DVE_SPLITS = (5, 13)
        POOL_SPLITS = [s for s in range(STEPS) if s not in DVE_SPLITS]

        def extra(i):
            return bank[5 + i % 3]

        def split_count(h, s):
            if s in DVE_SPLITS:
                return plow_dve, len(DVE_SPLITS) * h + DVE_SPLITS.index(s) + 1
            return plow_pool, len(POOL_SPLITS) * h + POOL_SPLITS.index(s) + 1

        block = ctx.enter_context(nc.Block())

        @block.sync
        def _(sp):
            for g in range(TG):
                sp.dma_start(x[:, g * TGW:(g + 1) * TGW].rearrange("p (n d) -> p n d", d=D),
                             z_t[:, g * TPG:(g + 1) * TPG, :]).then_inc(x_in[g], 16)
            sp.dma_start(gate32[:, :], gate_w).then_inc(gate_in, 16)
            sp.dma_start(rows[:, :], b1.rearrange("e (f p) -> (e f) p", p=P)).then_inc(rows_in, 16)
            for w, b in enumerate((fcq_b, fck_b)):
                for r in range(2):
                    sp.dma_start(qkrows[:, w, r * DK:(r + 1) * DK],
                                 b.rearrange("(h d) -> h d", d=DK)).then_inc(rows_in, 16)
            for c in range(4):
                sp.dma_start(w1_32[:, c * 1024:(c + 1) * 1024].rearrange("p (e f) -> p e f", f=F),
                             w1[2 * c:2 * c + 2].rearrange("e d f -> d e f")).then_inc(w1_in[c], 16)
            for c in range(4):
                sp.dma_start(w2_32[:, c * 1024:(c + 1) * 1024].rearrange("p (e f d) -> p e f d", f=FB, d=D),
                             w2[2 * c:2 * c + 2].rearrange("e (f p) d -> p e f d", p=P)).then_inc(w2_in[c], 16)
            for w, m in enumerate((wq, wk, wv)):
                sp.dma_start(pw32[:, w, :], m).then_inc(attn_in, 16)
            for r in range(2):
                for w, m in enumerate((fcq_w, fck_w)):
                    sp.dma_start(fqk_32[r * DK:(r + 1) * DK, w, :, :],
                                 m.rearrange("k (h d) -> k h d", d=DK)).then_inc(attn_in, 16)
                sp.dma_start(fv_32[r * DK:(r + 1) * DK, :], fcv_w).then_inc(attn_in, 16)
            sp.dma_start(fo_32.rearrange("p (k e) -> p k e", e=D),
                         fco_w.rearrange("(k p) e -> p k e", p=P)).then_inc(attn_in, 16)
            sp.dma_start(vbias[:, :], fcv_b.rearrange("(a n) -> a n", a=1).partition_broadcast(P)).then_inc(attn_in, 16)
            sp.dma_start(obias[:, :], fco_b.rearrange("(a n) -> a n", a=1).partition_broadcast(P)).then_inc(obias_in, 16)
            sp.wait_ge(b2_zeroed, 1)
            for n in range(NT):
                sp.dma_start(b2diag[n * E:(n + 1) * E, n * D:(n + 1) * D], b2).then_inc(b2_in, 16)
            sp.wait_ge(y_added, 2 * UNITS)
            for g in range(TG):
                sp.dma_start(out_t[:, g * TPG:(g + 1) * TPG, :],
                             x[:, g * TGW:(g + 1) * TGW].rearrange("p (n d) -> p n d", d=D)).then_inc(stored, 16)
            sp.wait_ge(stored, 16 * TG)

        ATTN_DMAS = 3 + 6 + 1 + 1

        @block.gpsimd
        def _(pool):
            pool.memset(ident[:, :], 0.0).then_inc(pool_step, 1)
            pool.memset(before[:, :, :], 1.0).then_inc(pool_step, 1)
            pool.memset(b2diag[:, :], 0.0).then_inc(b2_zeroed, 1)
            pool.wait_ge(pool_step, 2)
            pool.affine_select(out=ident[:, :], in_=ident[:, :], compare_op=ALU.not_equal, fill=1.0, base=0,
                               pattern=[[-1, P]], channel_multiplier=1).then_inc(ident_ready, 1)
            pool.affine_select(out=before[:, :, :], in_=before[:, :, :], compare_op=ALU.is_gt, fill=0.0, base=0,
                               pattern=[[1, E], [-1, E]], channel_multiplier=0).then_inc(before_ready, 1)
            pool.wait_ge(ident_ready, 1)
            pool.tensor_copy(ident16[:, :], ident[:, :]).then_inc(ident_ready, 1)
            for c in range(4):
                s = slice(c * 1024, (c + 1) * 1024)
                pool.wait_ge(w2h_ready, c + 1)
                pool.tensor_tensor(w2l[:, s], w2_32[:, s], w2h[:, s], ALU.subtract).then_inc(w2l_ready, 1)
            pool.wait_ge(ah_ready, 1)
            for r in range(2):
                pool.tensor_tensor(pwl[:, :, r, :], pw32[:, :, :], pwh[:, :, r, :], ALU.subtract)
                for w in range(2):
                    pool.tensor_tensor(fqk_l[:, w, :, r, :], fqk_32[:, w, :, :], fqk_h[:, w, :, r, :],
                                       ALU.subtract)
            pool.tensor_tensor(fv_l[:, :], fv_32, fv_h[:, :], ALU.subtract)
            pool.tensor_tensor(fo_l[:, :], fo_32, fo_h[:, :], ALU.subtract).then_inc(al_ready, 1)

            def moe(k):
                base = k * UNITS

                def pair(p):
                    for q in range(2):
                        n = base + 2 * p + q
                        for f in range(FB):
                            pool.wait_ge(hh_done, FB * n + f + 1)
                            pool.tensor_tensor(hl[q][f], g32[q][f], hh[q][f], ALU.subtract).then_inc(hl_done, 1)

                pair(0)
                with pool.Fori(1, UNITS // 2) as p:
                    pair(p)

            moe(0)
            pool.wait_ge(y_done, UNITS)
            for i in range(2):
                pool.memset(q2[i][DK:P, :], 0.0)
                last = pool.memset(k2[i][DK:P, :], 1.0)
            last.then_inc(pad_ready, 1)
            pool.wait_ge(pad_ready, 1)
            for i in range(2):
                last = pool.memset(vv[i][:, :, DK:DK + 1], 1.0)
            last.then_inc(pad_ready, 1)
            pool.wait_ge(pad_ready, 2)

            pool.wait_ge(obias_in, 16)
            pool.wait_ge(xn_ready, 2 * TG)
            pool.tensor_tensor(x[:, :].rearrange("p (n d) -> p n d", d=D),
                               x[:, :].rearrange("p (n d) -> p n d", d=D),
                               obias[:, :].unsqueeze(1).to_broadcast([P, NT, D]), ALU.add).then_inc(xbias_added, 1)

            def v_low(h, i):
                pool.wait_ge(v_hi, h + 1)
                pool.tensor_tensor(vv[i][:, :, DK + 1:VW], vsum[:, :, :], vv[i][:, :, 0:DK],
                                   ALU.subtract).then_inc(v_lo, 1)

            def head(h, i, last=False):
                for s in range(STEPS):
                    if s in POOL_SPLITS:
                        pool.wait_ge(exp_done, STEPS * h + s + 1)
                        hi = prob[s % 4].bitcast(BF16).rearrange("p (n t) -> p n t", t=2)[:, :, 1]
                        pool.tensor_tensor(plow[s % 4], prob[s % 4], hi, ALU.subtract).then_inc(plow_pool, 1)
                    if s == 4 and not last:
                        v_low(h + 1, 1 - i)

            v_low(0, 0)
            head(0, 0)
            head(1, 1)
            with pool.Fori(1, NH // 2 - 1) as p:
                head(2 * p, 0)
                head(2 * p + 1, 1)
            head(NH - 2, 0)
            head(NH - 1, 1, last=True)
            moe(1)

        @block.scalar
        def _(act):
            def turn_ln(n):
                act.wait_ge(var_ready, n + 1)
                act.activation(sd[:, :], var_eps[:, :], ACT.Sqrt).then_inc(sd_ready, 1)

            def ln_high(n, g):
                act.wait_ge(xn_turned, TG * n + g + 1)
                act.activation(xh[:, g * TGW:(g + 1) * TGW], bank[6 + g % 2], ACT.Copy).then_inc(xh_ready, 1)

            turn_ln(0)
            act.wait_ge(gate_in, 16)
            act.activation(gh[:, :], gate32[:, :], ACT.Copy).then_inc(gh_ready, 1)
            for g in range(TG):
                ln_high(0, g)
                act.wait_ge(w1_in[g], 16)
                s = slice(g * 1024, (g + 1) * 1024)
                act.activation(w1h[:, s], w1_32[:, s], ACT.Copy).then_inc(w1h_ready, 1)
            act.wait_ge(attn_in, 16 * ATTN_DMAS)
            for r in range(2):
                act.activation(pwh[:, :, r, :], pw32[:, :, :], ACT.Copy)
                for w in range(2):
                    act.activation(fqk_h[:, w, :, r, :], fqk_32[:, w, :, :], ACT.Copy)
            act.activation(fv_h[:, :], fv_32, ACT.Copy)
            act.activation(fo_h[:, :], fo_32, ACT.Copy).then_inc(ah_ready, 1)

            def moe(k):
                base = k * UNITS

                def gelu(p, q, f):
                    n = base + 2 * p + q
                    e = act.snap((2 * p + q) % E) if not isinstance(p, int) else (2 * p + q) % E
                    act.wait_ge(hid_done, FB * n + f + 1)
                    wait(act, hl_done, FB * (n - 2) + f + 1)
                    c = act.snap(e * FB + f) if not isinstance(e, int) else e * FB + f
                    act.activation(g32[q][f], bank[f], ACT.Gelu, bias=b1c[:, ds(c, 1)]).then_inc(gelu_done, 1)

                def pair(p):
                    for q in range(2):
                        for f in range(FB):
                            gelu(p, q, f)

                act.wait_ge(gap_ready, k + 1)
                act.activation(expgap[:, :], gap[:, :], ACT.Exp).then_inc(expgap_ready, 1)
                if k == 0:
                    act.wait_ge(bias_ready, 3)
                pair(0)
                with act.Fori(1, UNITS // 2) as p:
                    pair(p)

            moe(0)

            turn_ln(1)
            for g in range(TG):
                ln_high(1, g)
            for i in range(3 * TG):
                g, w = divmod(i, 3)
                act.wait_ge(u_done, i + 1)
                act.activation(u[w][:, g * TGW:(g + 1) * TGW], bank[i % 6][:, :], ACT.Copy).then_inc(uh_ready, 1)

            def fill(x_, i, f):
                kind, n = FILLS[f]
                half = slice(n * TGW, (n + 1) * TGW)
                if kind in "qk":
                    if f == 0:
                        hx = act.snap(x_ % H) if not isinstance(x_, int) else x_ % H
                        act.activation(hbias[i][:, :], qkbias[:, ds(hx, 1), :].rearrange("p h w -> p (h w)"),
                                       ACT.Copy).then_inc(hbias_ready, 1)
                        act.wait_ge(hbias_ready, x_ + 1)
                    dst, b = (q1, hbias[i][:, 0:1]) if kind == "q" else (k1, hbias[i][:, 1:2])
                    act.wait_ge(qk_done, 4 * x_ + f + 1)
                    act.activation(dst[i][:, half], extra(f)[:, :], ACT.Identity, bias=b).then_inc(qk_hi, 1)
                elif kind == "v":
                    act.wait_ge(v_ready32, x_ + 1)
                    act.activation(vv[i][:, :, 0:DK], vsum[:, :, :], ACT.Copy).then_inc(v_hi, 1)
                elif kind == "r":
                    act.wait_ge(mrow_done, 2 * x_ + n + 1)
                    act.activation(q2[i][DK:DK + 1, half], extra(f)[DK:DK + 1, :], ACT.Copy).then_inc(mrow_ready, 1)

            def copy_acc(h):
                act.wait_ge(pv_done, STEPS * (h + 1))
                wait(act, head_ready, h)
                for b, (lo, hi) in enumerate(((0, 3), (3, 6), (6, 8))):
                    last = act.activation(acc_sb[:, lo:hi, :],
                                          bank[b][:, 0:(hi - lo) * VW].rearrange("p (n c) -> p n c", c=VW),
                                          ACT.Copy)
                last.then_inc(acc_out, 1)

            def head(h, i, first=False, last=False):
                for s in range(STEPS):
                    if s == 1 and not first:
                        copy_acc(h - 1)
                    act.wait_ge(st_done, STEPS * h + s + 1)
                    wait(act, pv_done, STEPS * h + s - 3)
                    act.activation(prob[s % 4], bank[3 + s % 2][:, :], ACT.Exp, scale=SCALE).then_inc(exp_done, 1)
                    if not last:
                        for f in fills_at[s]:
                            fill(h + 1, 1 - i, f)

            for f in range(len(FILLS)):
                fill(0, 0, f)
            head(0, 0, first=True)
            head(1, 1)
            with act.Fori(1, NH // 2 - 1) as p:
                head(2 * p, 0)
                head(2 * p + 1, 1)
            head(NH - 2, 0)
            head(NH - 1, 1, last=True)
            copy_acc(NH - 1)

            def turned_high(n, i):
                for c in range(2):
                    act.wait_ge(o_turned, 2 * n + c + 1)
                    wait(act, o_done, n - 1)
                    act.activation(oh[i][:, c * TGW:(c + 1) * TGW], bank[2 * i + c][:, :], ACT.Copy).then_inc(oh_ready, 1)

            for i in range(2):
                turned_high(i, i)
            with act.Fori(1, NT // 2) as p:
                for i in range(2):
                    turned_high(2 * p + i, i)

            turn_ln(2)
            for g in range(TG):
                ln_high(2, g)
            moe(1)

        @block.tensor
        def _(pe):
            def mm3(dst, lh, ll, rh, rl, start=True, stop=True, inc=None):
                pe.matmul(dst, lh, rh, start=start, stop=False, skip_group_check=True)
                pe.matmul(dst, lh, rl, start=False, stop=False, skip_group_check=True)
                last = pe.matmul(dst, ll, rh, start=False, stop=stop, skip_group_check=True)
                if inc is not None:
                    last.then_inc(inc, 1)

            def turn_ln(n):
                for g in range(TG):
                    pe.wait_ge(xn_ready, TG * n + g + 1)
                    if g >= 2 or n > 0:
                        pe.wait_ge(xl_ready, TG * n + g - 1)
                    for t in range(TPG):
                        c = (g * TPG + t) * D
                        last = pe.transpose(bank[6 + g % 2][:, t * P:(t + 1) * P], xn[:, c:c + D], ident[:, :])
                    last.then_inc(xn_turned, 1)

            pe.wait_ge(ident_ready, 1)
            pe.wait_ge(rows_in, 16 * 5)
            pe.transpose(bank[5][:, 0:E * FB], rows[:, :], ident[0:E * FB, 0:E * FB])
            pe.transpose(bank[5][:, 32:32 + H], qkrows[:, 0, :], ident[0:H, 0:H])
            pe.transpose(bank[5][:, 64:64 + H], qkrows[:, 1, :], ident[0:H, 0:H]).then_inc(bias_turned, 1)
            turn_ln(0)

            def moe(k):
                base = k * UNITS
                if k == 0:
                    pe.wait_ge(gl_ready, 1)
                    pe.wait_ge(bias_ready, 3)
                pe.wait_ge(xl_ready, TG * (2 * k + 1))
                for n in range(NT):
                    t = slice(n * P, (n + 1) * P)
                    dst = bank[5][:, n * E:(n + 1) * E]
                    for a, (lhs, rhs) in enumerate(((xh, gh), (xh, gl), (xl, gh), (xl, gl))):
                        last = pe.matmul(dst, lhs[:, t], rhs[:, :], start=(n == 0 and a == 0), stop=(a == 3),
                                         skip_group_check=True)
                last.then_inc(logit_done, 1)
                if k == 0:
                    pe.wait_ge(w1h_ready, 4)
                    pe.wait_ge(w1l_ready, 4)

                def hidden(p, q, e, tg):
                    n = base + 2 * p + q
                    for f in range(FB):
                        wait(pe, gelu_done, FB * (n - 1) + f + 1)
                        c = ds(e * F + f * P, P)
                        t = ds(tg * TGW, TGW)
                        mm3(bank[f][:, :], w1h[:, c], w1l[:, c], xh[:, t], xl[:, t], inc=hid_done)

                def down(p, q, e):
                    n = base + 2 * p + q
                    wait(pe, y_added, n - 1)
                    if k == 0:
                        wait(pe, comb_ready, 1 if isinstance(p, int) and p == 0 else 0)
                    for f in range(FB):
                        pe.wait_ge(hl_done, FB * n + f + 1)
                        c = ds((e * FB + f) * D, D)
                        for t in range(TPG):
                            b = slice(t * P, (t + 1) * P)
                            mm3(bank[4 + q][:, b], hh[q][f][:, b], hl[q][f][:, b], w2h[:, c], w2l[:, c],
                                start=(f == 0 and t == 0), stop=(f == FB - 1),
                                inc=y_done if (f, t) == (FB - 1, TPG - 1) else None)

                def at(v):
                    if isinstance(v, int):
                        return v % E, v // E
                    return pe.snap(v % E), pe.snap(v // E)

                hidden(0, 0, *at(0))

                def pair(p, last=False):
                    e0, _ = at(2 * p)
                    e1, t1 = at(2 * p + 1)
                    hidden(p, 1, e1, t1)
                    down(p, 0, e0)
                    if not last:
                        e2, t2 = at(2 * p + 2)
                        hidden(p + 1, 0, e2, t2)
                    down(p, 1, e1)

                if k == 0:
                    pe.wait_ge(w2h_ready, 4)
                    pe.wait_ge(w2l_ready, 4)
                pair(0)
                with pe.Fori(1, UNITS // 2 - 1) as p:
                    pair(p)
                pe.wait_ge(comb_ready, k + 1)
                pe.transpose(bank[6][:, 0:P], comb[:, :, :].rearrange("p n e -> p (n e)"), ident[:, :]).then_inc(comb_turned, 1)
                pe.wait_ge(combT_ready, k + 1)
                if k == 0:
                    pe.wait_ge(b2_in, 16 * NT)
                for g in range(TG):
                    if g >= 1:
                        wait(pe, b2_added, TG * k + g - 1)
                    pe.matmul(bank[6 + (g + 1) % 2][:, :], combT[:, :], b2diag[:, g * TGW:(g + 1) * TGW],
                              start=True, stop=True).then_inc(b2_done, 1)
                pair(UNITS // 2 - 1, last=True)

            moe(0)

            turn_ln(1)
            pe.wait_ge(al_ready, 1)
            for i in range(3 * TG):
                g, w = divmod(i, 3)
                t = slice(g * TGW, (g + 1) * TGW)
                pe.wait_ge(xl_ready, TG + g + 1)
                wait(pe, ul_ready, i - 5)
                wh, wl = (m[:, w, :, :].rearrange("p r d -> p (r d)") for m in (pwh, pwl))
                mm3(bank[i % 6][:, :], wh, wl, xh[:, t], xl[:, t], inc=u_done)

            def fill(x_, i, f):
                kind, n = FILLS[f]
                dst = extra(f)
                g = f - 3 if f >= 3 else {0: 21, 1: 22, 2: 20}[f]
                y = x_ if f >= 3 else x_ - 1
                pk, pn = FILLS[g]
                s, v = {"q": (qk_lo, 4 * y + g + 1), "k": (qk_lo, 4 * y + g + 1), "v": (v_ready32, y + 1),
                        "m": (smax_red, STEPS * y + pn + 1), "r": (mrow_ready, 2 * y + pn + 1)}[pk]
                wait(pe, s, v)
                if kind in "qkv":
                    static = isinstance(x_, int)
                    hx = x_ % H if static else pe.snap(x_ % H)
                    bx = x_ // H if static else pe.snap(x_ // H)
                if kind in "qk":
                    w = "qk".index(kind)
                    uu = u[w][:, ds(bx * SEQ + n * TGW, TGW)]
                    fh, fl = (m[:, w, :, :, :].rearrange("p h r d -> p (h r d)")[:, ds(hx * P, P)]
                              for m in (fqk_h, fqk_l))
                    pe.matmul(dst[:, :], fh, uu, start=True, stop=False)
                    pe.matmul(dst[:, :], fl, uu, start=False, stop=True).then_inc(qk_done, 1)
                elif kind == "v":
                    c = ds(hx * DK, DK)
                    for j in range(JB):
                        uu = u[2][:, ds(bx * SEQ + j * P, P)]
                        pe.matmul(dst[:, j * DK:(j + 1) * DK], uu, fv_h[:, c], start=(j == 0), stop=False,
                                  skip_group_check=True)
                        last = pe.matmul(dst[:, j * DK:(j + 1) * DK], uu, fv_l[:, c], start=False, stop=True,
                                         skip_group_check=True)
                    last.then_inc(v_done, 1)
                elif kind == "m":
                    ib, half = divmod(n, 2)
                    if n == 0:
                        pe.wait_ge(qk_lo, 4 * x_ + 4)
                    pe.matmul(dst[:, :], q1[i][:, ib * P:(ib + 1) * P], k1[i][:, half * TGW:(half + 1) * TGW],
                              start=True, stop=True).then_inc(smax_done, 1)
                else:
                    if n == 0:
                        pe.wait_ge(negmax_ready, x_ + 1)
                    for t in range(TPG):
                        col = negmax[i][:, n * TPG + t:n * TPG + t + 1].to_broadcast([P, P])
                        last = pe.matmul(dst[:, t * P:(t + 1) * P], col, ident16[:, :], start=(t == 0), stop=True,
                                         skip_group_check=True)
                    last.then_inc(mrow_done, 1)

            def scores(h, i, s):
                j, half = divmod(s, 2)
                if s == 0:
                    pe.wait_ge(q2_hi, h + 1)
                    pe.wait_ge(mrow_ready, 2 * h + 2)
                wait(pe, exp_done, STEPS * h + s - 1)
                c, t = slice(j * P, (j + 1) * P), slice(half * TGW, (half + 1) * TGW)
                pe.matmul(bank[3 + s % 2][:, :], k1[i][:, c], q1[i][:, t], start=True, stop=False)
                pe.matmul(bank[3 + s % 2][:, :], k2[i][:, c], q2[i][:, t], start=False, stop=True).then_inc(st_done, 1)

            def values(h, i, s):
                j, half = divmod(s, 2)
                if s == 0:
                    wait(pe, acc_out, h)
                    pe.wait_ge(v_lo, h + 1)
                pe.wait_ge(*split_count(h, s))
                hi = prob[s % 4].bitcast(BF16).rearrange("p (n t) -> p n t", t=2)[:, :, 1]
                for t in range(TPG):
                    blk = half * TPG + t
                    dst = bank[blk // 3][:, blk % 3 * VW:(blk % 3 + 1) * VW]
                    c = slice(t * P, (t + 1) * P)
                    pe.matmul(dst, hi[:, c], vv[i][:, j, 0:VW], start=(j == 0 and blk % 3 == 0), stop=False,
                              skip_group_check=True)
                    last = pe.matmul(dst[:, 0:DK + 1], plow[s % 4][:, c], vv[i][:, j, 0:DK + 1], start=False,
                                     stop=(j == JB - 1), skip_group_check=True)
                last.then_inc(pv_done, 1)

            def head(h, i, first=False, last=False):
                for s in range(STEPS):
                    scores(h, i, s)
                    if not last:
                        for f in fills_at[s]:
                            fill(h + 1, 1 - i, f)
                    for dh, t in PV_AT[s]:
                        if not (first and dh < 0):
                            values(h + dh, (i + dh) % 2, t)

            pe.wait_ge(ul_ready, 3 * TG)
            pe.wait_ge(pad_ready, 2)
            for f in range(len(FILLS)):
                fill(0, 0, f)
            head(0, 0, first=True)
            head(1, 1)
            with pe.Fori(1, NH // 2 - 1) as p:
                head(2 * p, 0)
                head(2 * p + 1, 1)
            head(NH - 2, 0)
            head(NH - 1, 1, last=True)
            values(NH - 1, 1, STEPS - 2)
            values(NH - 1, 1, STEPS - 1)

            def turn_heads(n, i):
                wait(pe, ol_ready, 2 * n - 2)
                for c in range(2):
                    for t in range(TPG):
                        src = heads[:, :, :].rearrange("p n d -> p (n d)")[
                            :, ds(n * H * DK + (c * TPG + t) * P, P)]
                        last = pe.transpose(bank[2 * i + c][:, t * P:(t + 1) * P], src, ident[:, :])
                    last.then_inc(o_turned, 1)

            def project(n, i):
                wait(pe, o_added, n - 1)
                pe.wait_ge(ol_ready, 2 * n + 2)
                for c in range(PAIRS):
                    b = slice(c * P, (c + 1) * P)
                    mm3(bank[4 + i][:, 0:D], oh[i][:, b], ol[i][:, b], fo_h[:, b], fo_l[:, b], start=(c == 0),
                        stop=(c == PAIRS - 1), inc=o_done if c == PAIRS - 1 else None)

            def out_pair(p, last=False):
                turn_heads(2 * p + 1, 1)
                project(2 * p, 0)
                if not last:
                    turn_heads(2 * p + 2, 0)
                project(2 * p + 1, 1)

            pe.wait_ge(head_ready, NH)
            turn_heads(0, 0)
            for p in range(NT // 2):
                out_pair(p, last=p == NT // 2 - 1)

            turn_ln(2)
            moe(1)

        @block.vector
        def _(dve):
            steps = [0]

            def then(ins):
                steps[0] += 1
                ins.then_inc(dve_step, 1)
                dve.wait_ge(dve_step, steps[0])

            def layer_norm(n):
                for t in range(NT):
                    if n == 0 and t % TPG == 0:
                        dve.wait_ge(x_in[t // TPG], 16)
                    last = dve.bn_stats(stats[:, t, :], x[:, t * D:(t + 1) * D])
                then(last)
                for t in range(NT):
                    last = dve.bn_aggr(mv[:, t, :], stats[:, t, :])
                then(last)
                dve.tensor_scalar(var_eps[:, :], mv[:, :, 1], EPS, None, ALU.add).then_inc(var_ready, 1)
                dve.wait_ge(sd_ready, n + 1)
                then(dve.reciprocal(rstd[:, :], sd[:, :]))
                for g in range(TG):
                    if n > 0 and g == 0:
                        dve.wait_ge(xn_turned, TG * n)
                    for t in range(g * TPG, (g + 1) * TPG):
                        last = dve.tensor_scalar(xn[:, t * D:(t + 1) * D], x[:, t * D:(t + 1) * D], mv[:, t, 0:1],
                                                 rstd[:, t:t + 1], ALU.subtract, ALU.mult)
                    last.then_inc(xn_ready, 1)
                for g in range(TG):
                    s = slice(g * TGW, (g + 1) * TGW)
                    dve.wait_ge(xh_ready, TG * n + g + 1)
                    dve.tensor_tensor(xl[:, s], bank[6 + g % 2], xh[:, s], ALU.subtract).then_inc(xl_ready, 1)
                    if n == 0:
                        c = slice(g * 1024, (g + 1) * 1024)
                        dve.wait_ge(w1h_ready, g + 1)
                        dve.tensor_tensor(w1l[:, c], w1_32[:, c], w1h[:, c], ALU.subtract).then_inc(w1l_ready, 1)

            layer_norm(0)
            dve.wait_ge(gh_ready, 1)
            dve.tensor_tensor(gl[:, :], gate32[:, :], gh[:, :], ALU.subtract).then_inc(gl_ready, 1)
            dve.wait_ge(bias_turned, 1)
            dve.tensor_copy(b1c[:, :], bank[5][:, 0:E * FB]).then_inc(bias_ready, 1)
            dve.tensor_copy(qkbias[:, :, 0], bank[5][:, 32:32 + H]).then_inc(bias_ready, 1)
            dve.tensor_copy(qkbias[:, :, 1], bank[5][:, 64:64 + H]).then_inc(bias_ready, 1)
            for c in range(4):
                s = slice(c * 1024, (c + 1) * 1024)
                dve.wait_ge(w2_in[c], 16)
                dve.tensor_copy(w2h[:, s], w2_32[:, s]).then_inc(w2h_ready, 1)

            def router(k):
                dve.wait_ge(logit_done, k + 1)
                then(dve.tensor_copy(logit[:, :, :].rearrange("p n e -> p (n e)"), bank[5][:, 0:NT * E]))
                mine = logit[:, :, :].unsqueeze(3).to_broadcast([P, NT, E, E])
                other = logit[:, :, :].unsqueeze(2).to_broadcast([P, NT, E, E])
                above = xn[:, 0:NT * E * E].rearrange("p (n e o) -> p n e o", e=E, o=E)
                equal = xn[:, NT * E * E:2 * NT * E * E].rearrange("p (n e o) -> p n e o", e=E, o=E)
                dve.wait_ge(before_ready, 1)
                dve.tensor_tensor(above, other, mine, ALU.is_gt)
                then(dve.tensor_tensor(equal, other, mine, ALU.is_equal))
                then(dve.tensor_tensor(equal, equal, before[:, :, :].unsqueeze(1).to_broadcast([P, NT, E, E]), ALU.mult))
                then(dve.tensor_tensor(above, above, equal, ALU.add))
                then(dve.tensor_reduce(rank[:, :, :], above, AX.X, ALU.add))
                for r in range(2):
                    then(dve.tensor_scalar(sel[:, r, :, :], rank[:, :, :], float(r), None, ALU.is_equal))
                    then(dve.tensor_tensor(picked[:, :, :], sel[:, r, :, :], logit[:, :, :], ALU.mult))
                    then(dve.tensor_reduce(top[:, r, :], picked[:, :, :], AX.X, ALU.add))
                dve.tensor_tensor(gap[:, :], top[:, 1, :], top[:, 0, :], ALU.subtract).then_inc(gap_ready, 1)
                dve.wait_ge(expgap_ready, k + 1)
                then(dve.tensor_scalar(wtop[:, 0, :], expgap[:, :], 1.0, None, ALU.add))
                then(dve.reciprocal(wtop[:, 1, :], wtop[:, 0, :]))
                then(dve.tensor_tensor(wtop[:, 2, :], wtop[:, 1, :], expgap[:, :], ALU.mult))
                for r in range(2):
                    then(dve.tensor_tensor(sel[:, r, :, :], sel[:, r, :, :],
                                           wtop[:, 1 + r, :].unsqueeze(2).to_broadcast([P, NT, E]), ALU.mult))
                then(dve.tensor_tensor(picked[:, :, :], sel[:, 0, :, :], sel[:, 1, :, :], ALU.add))
                dve.tensor_scalar(comb[:, :, :], picked[:, :, :], 0.5, None, ALU.mult).then_inc(comb_ready, 1)
                dve.wait_ge(comb_ready, k + 1)

            def moe(k):
                base = k * UNITS
                router(k)

                def at(v):
                    if isinstance(v, int):
                        return v % E, v // E
                    return dve.snap(v % E), dve.snap(v // E)

                def high(p, q):
                    n = base + 2 * p + q
                    for f in range(FB):
                        dve.wait_ge(gelu_done, FB * n + f + 1)
                        if f == 0:
                            wait(dve, y_done, n - 1)
                        dve.tensor_copy(hh[q][f], g32[q][f]).then_inc(hh_done, 1)

                def add(v, q):
                    e, tg = at(v)
                    dve.wait_ge(y_done, base + v + 1)
                    wait(dve, y_added, base + v)
                    for t in range(TPG):
                        xs = x[:, ds((tg * TPG + t) * D, D)]
                        w = comb[:, :, :].rearrange("p n e -> p (n e)")[:, ds((tg * TPG + t) * E + e, 1)]
                        last = dve.scalar_tensor_tensor(out=xs, in0=bank[4 + q][:, t * P:(t + 1) * P], scalar=w,
                                                        in1=xs, op0=ALU.mult, op1=ALU.add)
                    last.then_inc(y_added, 1)

                def pair(p, first=False):
                    high(p, 0)
                    if not first:
                        add(2 * p - 1, 1)
                    high(p, 1)
                    add(2 * p, 0)

                pair(0, first=True)
                with dve.Fori(1, UNITS // 2 - 1) as p:
                    pair(p)
                dve.wait_ge(comb_turned, k + 1)
                dve.tensor_copy(combT[:, :], bank[6][:, 0:P]).then_inc(combT_ready, 1)
                dve.wait_ge(y_added, base + UNITS - 3)
                for g in range(TG):
                    s = slice(g * TGW, (g + 1) * TGW)
                    dve.wait_ge(b2_done, TG * k + g + 1)
                    last = dve.tensor_tensor(x[:, s], x[:, s], bank[6 + (g + 1) % 2], ALU.add)
                    last.then_inc(b2_added, 1)
                dve.wait_ge(b2_added, TG * (k + 1))
                pair(UNITS // 2 - 1)
                add(UNITS - 1, 1)
                dve.wait_ge(y_added, base + UNITS)

            moe(0)
            layer_norm(1)
            for i in range(3 * TG):
                g, w = divmod(i, 3)
                s = slice(g * TGW, (g + 1) * TGW)
                dve.wait_ge(uh_ready, i + 1)
                dve.tensor_tensor(u[w][DK:P, s], bank[i % 6][DK:P, :], u[w][DK:P, s], ALU.subtract).then_inc(ul_ready, 1)

            def fill(x_, i, f):
                kind, n = FILLS[f]
                half = slice(n * TGW, (n + 1) * TGW)
                if kind == "v":
                    hx = dve.snap(x_ % H) if not isinstance(x_, int) else x_ % H
                if kind in "qk":
                    dve.wait_ge(qk_hi, 4 * x_ + f + 1)
                    if kind == "q":
                        dve.scalar_tensor_tensor(out=q1[i][DK:P, half], in0=extra(f)[DK:P, :],
                                                 scalar=hbias[i][DK:P, 0:1], in1=q1[i][DK:P, half],
                                                 op0=ALU.add, op1=ALU.subtract).then_inc(qk_lo, 1)
                    else:
                        dve.scalar_tensor_tensor(out=k2[i][0:DK, half], in0=extra(f)[0:DK, :],
                                                 scalar=hbias[i][0:DK, 1:2], in1=k1[i][0:DK, half],
                                                 op0=ALU.add, op1=ALU.subtract).then_inc(qk_lo, 1)
                    if (kind, n) == ("q", 1):
                        dve.tensor_copy(q2[i][0:DK, :], q1[i][0:DK, :]).then_inc(q2_hi, 1)
                elif kind == "v":
                    dve.wait_ge(v_done, x_ + 1)
                    wait(dve, v_lo, x_)
                    bias = vbias[:, ds(hx * DK, DK)].unsqueeze(1).to_broadcast([P, JB, DK])
                    dve.tensor_tensor(vsum[:, :, :], extra(f)[:, :].rearrange("p (j d) -> p j d", d=DK), bias,
                                      ALU.add).then_inc(v_ready32, 1)
                elif kind == "m":
                    dve.wait_ge(smax_done, STEPS * x_ + n + 1)
                    dve.tensor_reduce(tilemax[i][:, n:n + 1], extra(f)[:, :], AX.X, ALU.max).then_inc(smax_red, 1)
                    if n == STEPS - 1:
                        dve.wait_ge(smax_red, STEPS * (x_ + 1))
                        wait(dve, mrow_done, 2 * x_ - 2)
                        dve.tensor_reduce(negmax[i][:, :], tilemax[i][:, :].rearrange("p (b h) -> p b h", h=2),
                                          AX.X, ALU.max, negate=True).then_inc(negmax_ready, 1)

            def normalise(h):
                if isinstance(h, int):
                    hx, bx = h % H, h // H
                else:
                    hx, bx = dve.snap(h % H), dve.snap(h // H)
                dve.wait_ge(acc_out, h + 1)
                dve.reciprocal(rsum[:, :], acc_sb[:, :, DK])
                dve.tensor_tensor(acc_sb[:, :, 0:DK], acc_sb[:, :, 0:DK], acc_sb[:, :, DK + 1:VW], ALU.add).then_inc(norm_step, 1)
                dve.wait_ge(norm_step, h + 1)
                dst = heads[:, ds(bx * JB, JB), ds(hx * DK, DK)]
                dve.tensor_tensor(dst, acc_sb[:, :, 0:DK], rsum[:, :].unsqueeze(2).to_broadcast([P, JB, DK]),
                                  ALU.mult).then_inc(head_ready, 1)

            def head(h, i, first=False, last=False):
                for s in range(STEPS):
                    if s == 3 and not first:
                        normalise(h - 1)
                    if s in DVE_SPLITS:
                        dve.wait_ge(exp_done, STEPS * h + s + 1)
                        hi = prob[s % 4].bitcast(BF16).rearrange("p (n t) -> p n t", t=2)[:, :, 1]
                        dve.tensor_tensor(plow[s % 4], prob[s % 4], hi, ALU.subtract).then_inc(plow_dve, 1)
                    if not last:
                        for f in fills_at[s]:
                            fill(h + 1, 1 - i, f)

            for f in range(len(FILLS)):
                fill(0, 0, f)
            head(0, 0, first=True)
            head(1, 1)
            with dve.Fori(1, NH // 2 - 1) as p:
                head(2 * p, 0)
                head(2 * p + 1, 1)
            head(NH - 2, 0)
            head(NH - 1, 1, last=True)
            normalise(NH - 1)

            def turned_low(n, i):
                for c in range(2):
                    b = slice(c * TGW, (c + 1) * TGW)
                    dve.wait_ge(oh_ready, 2 * n + c + 1)
                    dve.tensor_tensor(ol[i][:, b], bank[2 * i + c][:, :], oh[i][:, b], ALU.subtract).then_inc(ol_ready, 1)

            def add_out(n, i):
                dve.wait_ge(o_done, n + 1)
                xs = x[:, ds(n * D, D)]
                dve.tensor_tensor(xs, xs, bank[4 + i][:, 0:D], ALU.add).then_inc(o_added, 1)

            def out_pair(p, first=False):
                turned_low(2 * p, 0)
                if not first:
                    add_out(2 * p - 1, 1)
                turned_low(2 * p + 1, 1)
                add_out(2 * p, 0)

            dve.wait_ge(xbias_added, 1)
            out_pair(0, first=True)
            with dve.Fori(1, NT // 2) as p:
                out_pair(p)
            add_out(NT - 1, 1)
            dve.wait_ge(o_added, NT)
            layer_norm(2)
            moe(1)


_INS = ["attn_z", "attn_wq", "attn_wk", "attn_wv", "attn_fcq_w", "attn_fcq_b", "attn_fck_w", "attn_fck_b",
        "attn_fcv_w", "attn_fcv_b", "attn_fco_w", "attn_fco_b", "ffn_gate_w", "ffn_w1", "ffn_b1", "ffn_w2", "ffn_b2"]


def kernel(**inputs):
    import numpy as np
    import concourse.bacc as bacc
    from concourse.bass_utils import run_bass_kernel_spmd

    nc = bacc.Bacc("TRN2", target_bir_lowering=False, num_devices=1)
    arrays, args = {}, []
    for name in _INS:
        a = np.ascontiguousarray(inputs[f"L0_{name}"])
        arrays[name] = a
        args.append(nc.dram_tensor(name, a.shape, mybir.dt.from_np(a.dtype), kind="ExternalInput").ap())
    y = nc.dram_tensor("y", arrays["attn_z"].shape, F32, kind="ExternalOutput").ap()
    macaron_block(nc, *args, y)
    result = run_bass_kernel_spmd(nc, [arrays], core_ids=[0])
    return result.results[0]["y"]
```

```python
from contextlib import ExitStack

import concourse.bass as bass
from concourse import mybir

F32 = mybir.dt.float32
F16 = mybir.dt.float16
BF16 = mybir.dt.bfloat16
ACT = mybir.ActivationFunctionType
ALU = mybir.AluOpType
AX = mybir.AxisListType
ds = bass.ds


def macaron_block(nc, z, wq, wk, wv, fcq_w, fcq_b, fck_w, fck_b, fcv_w, fcv_b, fco_w, fco_b,
                  gate_w, w1, b1, w2, b2, out):
    P = 128
    BATCH, SEQ, D = z.shape
    T = BATCH * SEQ
    NT = T // P
    TGW = 512
    TG = T // TGW
    TPG = TGW // P
    E, _, F = w1.shape
    FB = F // P
    DK = wq.shape[1]
    H = fcq_w.shape[1] // DK
    NH = BATCH * H
    JB = SEQ // P
    HALVES = SEQ // TGW
    STEPS = JB * HALVES
    VW = 2 * DK + 1
    PAIRS = H * DK // P
    UNITS = TG * E
    EPS = 1e-5
    SCALE = float(DK) ** -0.5
    assert (D, DK, F, JB, STEPS) == (128, 64, 512, 8, 16)

    z_t = z.rearrange("b (n p) d -> p (b n) d", p=P)
    out_t = out.rearrange("b (n p) d -> p (b n) d", p=P)

    with ExitStack() as ctx:
        def sb(name, shape, dt):
            return ctx.enter_context(nc.sbuf_tensor(name, shape, dt))

        def sem(name):
            return ctx.enter_context(nc.semaphore(name))

        bank = [ctx.enter_context(nc.psum_tensor(f"bank{i}", [P, 512], F32))[:, :] for i in range(6)]
        duo = ctx.enter_context(nc.psum_tensor("duo", [P, 2, 512], F32))
        bank += [duo[:, 0, :], duo[:, 1, :]]

        x = sb("x", [P, NT * D], F32)
        xh = sb("xh", [P, T], F16)
        xl = sb("xl", [P, T], F16)
        w1h = sb("w1h", [P, E * F], F16)
        w1l = sb("w1l", [P, E * F], F16)
        w2h = sb("w2h", [P, E * FB * D], F16)
        w2l = sb("w2l", [P, E * FB * D], F16)
        b1c = sb("b1c", [P, E * FB], F32)
        gh = sb("gh", [P, E], F16)
        gl = sb("gl", [P, E], F16)
        gate32 = sb("gate32", [P, E], F32)
        ident = sb("ident", [P, P], F32)
        ident16 = sb("ident16", [P, P], F16)
        before = sb("before", [P, E, E], F32)
        qkbias = sb("qkbias", [P, H, 2], F32)
        hbias = [sb(f"hbias{i}", [P, 2], F32) for i in range(2)]
        vbias = sb("vbias", [P, PAIRS], F32)
        vbias_h = sb("vbias_h", [P, PAIRS], F16)
        vbias_l = sb("vbias_l", [P, PAIRS], F16)
        obias = sb("obias", [P, D], F32)
        pw32 = sb("pw32", [P, 3, DK], F32)
        pwh = sb("pwh", [P, 3, 2, DK], F16)
        pwl = sb("pwl", [P, 3, 2, DK], F16)
        fqk_h = sb("fqk_h", [P, 2, H, 2, DK], F16)
        fqk_l = sb("fqk_l", [P, 2, H, 2, DK], F16)
        fv_h = sb("fv_h", [P, H * DK], F16)
        fv_l = sb("fv_l", [P, H * DK], F16)
        fo_h = sb("fo_h", [P, PAIRS * D], F16)
        fo_l = sb("fo_l", [P, PAIRS * D], F16)
        u = [sb(f"u{n}", [P, T], F16) for n in "qkv"]

        stats = sb("stats", [P, NT, 6], F32)
        mv = sb("mv", [P, NT, 2], F32)
        var_eps = sb("var_eps", [P, NT], F32)
        sd = sb("sd", [P, NT], F32)
        rstd = sb("rstd", [P, NT], F32)
        logit = sb("logit", [P, NT, E], F32)
        rank = sb("rank", [P, NT, E], F32)
        sel = sb("sel", [P, 2, NT, E], F32)
        picked = sb("picked", [P, NT, E], F32)
        top = sb("top", [P, 2, NT], F32)
        gap = sb("gap", [P, NT], F32)
        expgap = sb("expgap", [P, NT], F32)
        wtop = sb("wtop", [P, 3, NT], F32)
        comb = sb("comb", [P, NT, E], F32)
        combT = sb("combT", [P, P], F32)

        heads = sb("heads", [P, NT, H * DK], F32)
        stage = heads[:, :, :].rearrange("p n d -> p (n d)")
        w1_32 = stage[:, 0:E * F]
        b2diag = stage[:, 0:NT * D]
        w2_32 = stage[:, E * F:2 * E * F]
        fqk_32 = stage[:, 2 * E * F:2 * E * F + 2 * H * DK].rearrange("p (w h d) -> p w h d", w=2, h=H)
        fv_32 = stage[:, 2 * E * F + 2 * H * DK:2 * E * F + 3 * H * DK]
        fo_32 = stage[:, 2 * E * F + 3 * H * DK:2 * E * F + 4 * H * DK]

        work = sb("work", [P, 8256], F32)

        def view(a, n, dt=F32):
            v = work[:, a:a + n]
            return v if dt == F32 else v.bitcast(dt)

        g32 = [[view((2 * q + 0) * 1024 + 512 * f if f < 2 else (2 * q + 1) * 1024 + 512 * (f - 2), 512)
                for f in range(FB)] for q in range(2)]
        hh = [[view(4096 + 1024 * q + 256 * f, 256, F16) for f in range(FB)] for q in range(2)]
        hl = [[view(6144 + 1024 * q + 256 * f, 256, F16) for f in range(FB)] for q in range(2)]

        xn = view(6144, NT * D)
        rows = work[0:E * FB, 0:P]
        vrows = work[0:PAIRS, 3 * P:4 * P]
        qkrows = work[0:H, P:3 * P].rearrange("p (w c) -> p w c", w=2)

        q1 = [view(2048 * i, 512, F16) for i in range(2)]
        q2 = [view(2048 * i + 512, 512, F16) for i in range(2)]
        k1 = [view(2048 * i + 1024, 512, F16) for i in range(2)]
        k2 = [view(2048 * i + 1536, 512, F16) for i in range(2)]
        VPITCH = 132
        vv = [view(4096 + i * JB * VPITCH // 2, JB * VPITCH // 2, F16)
              .rearrange("p (j c) -> p j c", j=JB) for i in range(2)]
        prob = [view(5184 + 512 * i, 512) for i in range(4)]
        prob += [t[:, TGW * 2 * i:TGW * 2 * (i + 1)].bitcast(F32) for t in (xh, xl) for i in range(2)]
        plow = [view(7232 + 256 * i, 256, F16) for i in range(4)]
        plow += [sb(f"plow{i}", [P, TGW], F16)[:, :] for i in range(4)]
        RING = len(prob)
        acc_sb = sb("acc_sb", [P, JB, VW], F32)
        rsum = sb("rsum", [P, JB], F32)
        tilemax = [sb(f"tilemax{i}", [P, STEPS], F32) for i in range(2)]
        negmax = [sb(f"negmax{i}", [P, JB], F16) for i in range(2)]
        oh = [view(1024 * i, 512, F16) for i in range(2)]
        ol = [view(1024 * i + 512, 512, F16) for i in range(2)]

        x_in = [sem(f"x_in{i}") for i in range(TG)]
        w1_in = [sem(f"w1_in{i}") for i in range(4)]
        w2_in = [sem(f"w2_in{i}") for i in range(4)]
        gate_in, rows_in, b2_in, attn_in, obias_in = (sem(n) for n in ("gate_in", "rows_in", "b2_in", "attn_in", "obias_in"))
        ident_ready, before_ready, b2_zeroed, pad_ready = (sem(n) for n in ("ident_ready", "before_ready", "b2_zeroed", "pad_ready"))
        w1h_ready, w1l_ready, w2h_ready, w2l_ready = (sem(n) for n in ("w1h_ready", "w1l_ready", "w2h_ready", "w2l_ready"))
        gh_ready, gl_ready, ah_ready, al_ready = (sem(n) for n in ("gh_ready", "gl_ready", "ah_ready", "al_ready"))
        bias_turned, bias_ready = sem("bias_turned"), sem("bias_ready")
        var_ready, sd_ready, xn_ready, xn_turned, xh_ready, xl_ready = (
            sem(n) for n in ("var_ready", "sd_ready", "xn_ready", "xn_turned", "xh_ready", "xl_ready"))
        logit_done, gap_ready, expgap_ready, comb_ready, comb_turned, combT_ready, b2_done, b2_added = (
            sem(n) for n in ("logit_done", "gap_ready", "expgap_ready", "comb_ready", "comb_turned", "combT_ready", "b2_done", "b2_added"))
        hid_done, gelu_done, hh_done, hl_done, y_done, y_added = (
            sem(n) for n in ("hid_done", "gelu_done", "hh_done", "hl_done", "y_done", "y_added"))
        u_done, uh_ready, ul_ready = (sem(n) for n in ("u_done", "uh_ready", "ul_ready"))
        qk_done, qk_hi, qk_lo, q2_hi, v_done, v_hi, v_lo = (
            sem(n) for n in ("qk_done", "qk_hi", "qk_lo", "q2_hi", "v_done", "v_hi", "v_lo"))
        smax_done, smax_red, negmax_ready, mrow_done, mrow_ready = (
            sem(n) for n in ("smax_done", "smax_red", "negmax_ready", "mrow_done", "mrow_ready"))
        st_done, exp_done, plow_pool, plow_dve, pv_done, acc_out, head_ready = (
            sem(n) for n in ("st_done", "exp_done", "plow_pool", "plow_dve", "pv_done", "acc_out", "head_ready"))
        o_turned, oh_ready, ol_ready, o_done, o_added, xbias_added = (
            sem(n) for n in ("o_turned", "oh_ready", "ol_ready", "o_done", "o_added", "xbias_added"))
        vbias_done, obias_ready, acc_sum = sem("vbias_done"), sem("obias_ready"), sem("acc_sum")
        norm_step, hbias_ready = sem("norm_step"), sem("hbias_ready")
        dve_step, pool_step, stored = sem("dve_step"), sem("pool_step"), sem("stored")

        def wait(eng, s, v):
            if not (isinstance(v, int) and v <= 0):
                eng.wait_ge(s, v)

        FILLS = [('q', 0), ('k', 0), ('q', 1), ('k', 1), ('m', 0), ('m', 1), ('m', 2), ('m', 3), ('m', 4), ('m', 5), ('m', 6), ('m', 7), ('m', 8), ('m', 9), ('m', 10), ('m', 11), ('m', 12), ('m', 13), ('m', 14), ('m', 15), ('v', 0), ('r', 0), ('r', 1)]
        PE_FILLS = [([], [0]), ([], [1, 2]), ([], []), ([3], [4]), ([], [5]), ([6], [7, 8]), ([], [9]), ([10], [11]), ([12], []), ([13, 14], []), ([], [15, 16]), ([], [17]), ([18], [19]), ([], []), ([20, 21], [22]), ([], [])]
        ACT_FILLS = [[0], [1, 2], [3, 4, 5], [], [6, 7], [], [8, 9, 10, 11, 12], [], [13, 14], [15], [16], [], [17], [18, 19], [20, 21, 22], []]
        DVE_FILLS = [[0, 1, 2], [3, 4, 5, 6, 7], [8, 9, 10], [11, 12, 13, 14], [], [], [], [15, 16], [17, 18, 19], [20], [], [21], [], [], [22], []]
        PV_AT = [[], [-6, -5], [], [-4, -3, -2, -1], [], [0, 1], [2], [3], [], [4], [], [5], [], [6], [7], [8, 9]]
        ACC_STEP, ADD_STEP, NORM_STEP = (4, 13, 9)
        DVE_SPLITS = (0, 10, 12)
        POOL_SPLITS = [s for s in range(STEPS) if s not in DVE_SPLITS]

        QK = [f for f, (kind, _) in enumerate(FILLS) if kind in "qk"]

        def extra(i):
            return bank[5 + i % 3]

        def run_heads(eng, head):
            head(0, 0, 0, first=True)
            head(1, 1, 0)
            for b in range(BATCH):
                with eng.Fori(max(1, b * H // 2), (b + 1) * H // 2 - 1) as p:
                    head(2 * p, 0, b)
                    head(2 * p + 1, 1, b)
                head((b + 1) * H - 2, 0, b)
                head((b + 1) * H - 1, 1, b + 1, last=b == BATCH - 1)

        def column(eng, x_, b):
            return x_ - b * H if isinstance(x_, int) else eng.snap(x_ - b * H)

        def split_count(h, s):
            if s in DVE_SPLITS:
                return plow_dve, len(DVE_SPLITS) * h + DVE_SPLITS.index(s) + 1
            return plow_pool, len(POOL_SPLITS) * h + POOL_SPLITS.index(s) + 1

        block = ctx.enter_context(nc.Block())

        @block.sync
        def _(sp):
            for g in range(TG):
                sp.dma_start(x[:, g * TGW:(g + 1) * TGW].rearrange("p (n d) -> p n d", d=D),
                             z_t[:, g * TPG:(g + 1) * TPG, :]).then_inc(x_in[g], 16)
            sp.dma_start(gate32[:, :], gate_w).then_inc(gate_in, 16)
            sp.dma_start(rows[:, :], b1.rearrange("e (f p) -> (e f) p", p=P)).then_inc(rows_in, 16)
            for w, b in enumerate((fcq_b, fck_b)):
                for r in range(2):
                    sp.dma_start(qkrows[:, w, r * DK:(r + 1) * DK],
                                 b.rearrange("(h d) -> h d", d=DK)).then_inc(rows_in, 16)
            sp.dma_start(vrows, fcv_b.rearrange("(k p) -> k p", p=P)).then_inc(rows_in, 16)
            for c in range(4):
                sp.dma_start(w1_32[:, c * 1024:(c + 1) * 1024].rearrange("p (e f) -> p e f", f=F),
                             w1[2 * c:2 * c + 2].rearrange("e d f -> d e f")).then_inc(w1_in[c], 16)
            for c in range(4):
                sp.dma_start(w2_32[:, c * 1024:(c + 1) * 1024].rearrange("p (e f d) -> p e f d", f=FB, d=D),
                             w2[2 * c:2 * c + 2].rearrange("e (f p) d -> p e f d", p=P)).then_inc(w2_in[c], 16)
            for w, m in enumerate((wq, wk, wv)):
                sp.dma_start(pw32[:, w, :], m).then_inc(attn_in, 16)
            for r in range(2):
                for w, m in enumerate((fcq_w, fck_w)):
                    sp.dma_start(fqk_32[r * DK:(r + 1) * DK, w, :, :],
                                 m.rearrange("k (h d) -> k h d", d=DK)).then_inc(attn_in, 16)
                sp.dma_start(fv_32[r * DK:(r + 1) * DK, :], fcv_w).then_inc(attn_in, 16)
            sp.dma_start(fo_32.rearrange("p (k e) -> p k e", e=D),
                         fco_w.rearrange("(k p) e -> p k e", p=P)).then_inc(attn_in, 16)
            sp.dma_start(obias[:, :], fco_b.rearrange("(a n) -> a n", a=1).partition_broadcast(P)).then_inc(obias_in, 16)
            for k in range(2):
                sp.wait_ge(b2_zeroed, k + 1)
                for n in range(NT):
                    sp.dma_start(b2diag[n * E:(n + 1) * E, n * D:(n + 1) * D], b2).then_inc(b2_in, 16)
            sp.wait_ge(y_added, 2 * UNITS)
            for g in range(TG):
                sp.dma_start(out_t[:, g * TPG:(g + 1) * TPG, :],
                             x[:, g * TGW:(g + 1) * TGW].rearrange("p (n d) -> p n d", d=D)).then_inc(stored, 16)
            sp.wait_ge(stored, 16 * TG)

        ATTN_DMAS = 3 + 6 + 1

        @block.gpsimd
        def _(pool):
            pool.memset(ident[:, :], 0.0).then_inc(pool_step, 1)
            pool.memset(before[:, :, :], 1.0).then_inc(pool_step, 1)
            pool.wait_ge(pool_step, 2)
            pool.affine_select(out=ident[:, :], in_=ident[:, :], compare_op=ALU.not_equal, fill=1.0, base=0,
                               pattern=[[-1, P]], channel_multiplier=1).then_inc(ident_ready, 1)
            pool.affine_select(out=before[:, :, :], in_=before[:, :, :], compare_op=ALU.is_gt, fill=0.0, base=0,
                               pattern=[[1, E], [-1, E]], channel_multiplier=0).then_inc(before_ready, 1)
            pool.wait_ge(ident_ready, 1)
            pool.tensor_copy(ident16[:, :], ident[:, :]).then_inc(ident_ready, 1)
            for c in range(4):
                s = slice(c * 1024, (c + 1) * 1024)
                pool.wait_ge(w2h_ready, c + 1)
                pool.tensor_tensor(w2l[:, s], w2_32[:, s], w2h[:, s], ALU.subtract).then_inc(w2l_ready, 1)
            pool.wait_ge(w1l_ready, 4)
            pool.memset(b2diag, 0.0).then_inc(b2_zeroed, 1)
            pool.wait_ge(ah_ready, 1)
            for r in range(2):
                pool.tensor_tensor(pwl[:, :, r, :], pw32[:, :, :], pwh[:, :, r, :], ALU.subtract)
                for w in range(2):
                    pool.tensor_tensor(fqk_l[:, w, :, r, :], fqk_32[:, w, :, :], fqk_h[:, w, :, r, :],
                                       ALU.subtract)
            pool.tensor_tensor(fv_l[:, :], fv_32, fv_h[:, :], ALU.subtract)
            pool.tensor_tensor(fo_l[:, :], fo_32, fo_h[:, :], ALU.subtract).then_inc(al_ready, 1)

            def moe(k):
                base = k * UNITS

                def pair(p):
                    for q in range(2):
                        n = base + 2 * p + q
                        for f in range(FB):
                            pool.wait_ge(hh_done, FB * n + f + 1)
                            pool.tensor_tensor(hl[q][f], g32[q][f], hh[q][f], ALU.subtract).then_inc(hl_done, 1)

                pair(0)
                with pool.Fori(1, UNITS // 2) as p:
                    pair(p)

            moe(0)
            pool.wait_ge(y_done, UNITS)
            for i in range(2):
                pool.memset(q2[i][DK:P, :], 0.0)
                last = pool.memset(k2[i][DK:P, :], 1.0)
            last.then_inc(pad_ready, 1)
            pool.wait_ge(pad_ready, 1)
            for i in range(2):
                last = pool.memset(vv[i][:, :, DK:DK + 1], 1.0)
            last.then_inc(pad_ready, 1)
            pool.wait_ge(pad_ready, 2)

            pool.wait_ge(obias_ready, 1)
            pool.wait_ge(xn_ready, 2 * TG)
            pool.tensor_tensor(x[:, :].rearrange("p (n d) -> p n d", d=D),
                               x[:, :].rearrange("p (n d) -> p n d", d=D),
                               obias[:, :].unsqueeze(1).to_broadcast([P, NT, D]), ALU.add).then_inc(xbias_added, 1)

            def add_acc(h):
                pool.wait_ge(acc_out, h + 1)
                pool.tensor_tensor(acc_sb[:, :, 0:DK], acc_sb[:, :, 0:DK], acc_sb[:, :, DK + 1:VW],
                                   ALU.add).then_inc(acc_sum, 1)

            def head(h, i, b, first=False, last=False):
                for s in range(STEPS):
                    if s == ADD_STEP and not first:
                        add_acc(h - 1)
                    if s in POOL_SPLITS:
                        pool.wait_ge(exp_done, STEPS * h + s + 1)
                        hi = prob[s % RING].bitcast(BF16).rearrange("p (n t) -> p n t", t=2)[:, :, 1]
                        pool.tensor_tensor(plow[s % RING], prob[s % RING], hi, ALU.subtract).then_inc(plow_pool, 1)

            run_heads(pool, head)
            add_acc(NH - 1)
            pool.wait_ge(o_turned, 2 * NT)
            pool.memset(b2diag, 0.0).then_inc(b2_zeroed, 1)
            moe(1)

        @block.scalar
        def _(act):
            def turn_ln(n):
                act.wait_ge(var_ready, n + 1)
                act.activation(sd[:, :], var_eps[:, :], ACT.Sqrt).then_inc(sd_ready, 1)

            def ln_high(n, g):
                act.wait_ge(xn_turned, TG * n + g + 1)
                act.activation(xh[:, g * TGW:(g + 1) * TGW], bank[6 + g % 2], ACT.Copy).then_inc(xh_ready, 1)

            turn_ln(0)
            act.wait_ge(gate_in, 16)
            act.activation(gh[:, :], gate32[:, :], ACT.Copy).then_inc(gh_ready, 1)
            for g in range(TG):
                ln_high(0, g)
                act.wait_ge(w1_in[g], 16)
                s = slice(g * 1024, (g + 1) * 1024)
                act.activation(w1h[:, s], w1_32[:, s], ACT.Copy).then_inc(w1h_ready, 1)
            act.wait_ge(attn_in, 16 * ATTN_DMAS)
            for r in range(2):
                act.activation(pwh[:, :, r, :], pw32[:, :, :], ACT.Copy)
                for w in range(2):
                    act.activation(fqk_h[:, w, :, r, :], fqk_32[:, w, :, :], ACT.Copy)
            act.activation(fv_h[:, :], fv_32, ACT.Copy)
            act.activation(fo_h[:, :], fo_32, ACT.Copy).then_inc(ah_ready, 1)

            def moe(k):
                base = k * UNITS

                def gelu(p, q, f):
                    n = base + 2 * p + q
                    e = act.snap((2 * p + q) % E) if not isinstance(p, int) else (2 * p + q) % E
                    act.wait_ge(hid_done, FB * n + f + 1)
                    wait(act, hl_done, FB * (n - 2) + f + 1)
                    c = act.snap(e * FB + f) if not isinstance(e, int) else e * FB + f
                    act.activation(g32[q][f], bank[f], ACT.Gelu, bias=b1c[:, ds(c, 1)]).then_inc(gelu_done, 1)

                def pair(p):
                    for q in range(2):
                        for f in range(FB):
                            gelu(p, q, f)

                act.wait_ge(gap_ready, k + 1)
                act.activation(expgap[:, :], gap[:, :], ACT.Exp).then_inc(expgap_ready, 1)
                if k == 0:
                    act.wait_ge(bias_ready, 6)
                pair(0)
                with act.Fori(1, UNITS // 2) as p:
                    pair(p)

            moe(0)

            turn_ln(1)
            for g in range(TG):
                ln_high(1, g)
            for i in range(3 * TG):
                g, w = divmod(i, 3)
                act.wait_ge(u_done, i + 1)
                act.activation(u[w][:, g * TGW:(g + 1) * TGW], bank[i % 6][:, :], ACT.Copy).then_inc(uh_ready, 1)

            def fill(x_, i, f, b):
                kind, n = FILLS[f]
                half = slice(n * TGW, (n + 1) * TGW)
                if kind in "qk":
                    if f == 0:
                        hx = column(act, x_, b)
                        act.activation(hbias[i][:, :], qkbias[:, ds(hx, 1), :].rearrange("p h w -> p (h w)"),
                                       ACT.Copy).then_inc(hbias_ready, 1)
                        act.wait_ge(hbias_ready, x_ + 1)
                    dst, bias = (q1, hbias[i][:, 0:1]) if kind == "q" else (k1, hbias[i][:, 1:2])
                    act.wait_ge(qk_done, 4 * x_ + QK.index(f) + 1)
                    act.activation(dst[i][:, half], extra(f), ACT.Identity, bias=bias).then_inc(qk_hi, 1)
                    if kind == "q":
                        act.activation(q2[i][0:DK, half], extra(f)[0:DK, :], ACT.Identity,
                                       bias=bias[0:DK, :]).then_inc(q2_hi, 1)
                elif kind == "v":
                    act.wait_ge(v_done, x_ + 1)
                    act.activation(vv[i][:, :, 0:DK], extra(f).rearrange("p (j d) -> p j d", d=DK),
                                   ACT.Copy).then_inc(v_hi, 1)
                elif kind == "r":
                    act.wait_ge(mrow_done, 2 * x_ + n + 1)
                    act.activation(q2[i][DK:DK + 1, half], extra(f)[DK:DK + 1, :], ACT.Copy).then_inc(mrow_ready, 1)

            def copy_acc(h):
                act.wait_ge(pv_done, STEPS * (h + 1))
                wait(act, head_ready, h)
                for b, (lo, hi) in enumerate(((0, 3), (3, 6), (6, 8))):
                    last = act.activation(acc_sb[:, lo:hi, :],
                                          bank[b][:, 0:(hi - lo) * VW].rearrange("p (n c) -> p n c", c=VW),
                                          ACT.Copy)
                last.then_inc(acc_out, 1)

            def head(h, i, b, first=False, last=False):
                for s in range(STEPS):
                    if s == ACC_STEP and not first:
                        copy_acc(h - 1)
                    act.wait_ge(st_done, STEPS * h + s + 1)
                    wait(act, pv_done, STEPS * h + s + 1 - RING)
                    act.activation(prob[s % RING], bank[3 + s % 2][:, :], ACT.Exp, scale=SCALE).then_inc(exp_done, 1)
                    if not last:
                        for f in ACT_FILLS[s]:
                            fill(h + 1, 1 - i, f, b)

            for f in range(len(FILLS)):
                fill(0, 0, f, 0)
            run_heads(act, head)
            copy_acc(NH - 1)

            def turned_high(n, i):
                for c in range(2):
                    act.wait_ge(o_turned, 2 * n + c + 1)
                    wait(act, o_done, n - 1)
                    act.activation(oh[i][:, c * TGW:(c + 1) * TGW], bank[2 * i + c][:, :], ACT.Copy).then_inc(oh_ready, 1)

            for i in range(2):
                turned_high(i, i)
            with act.Fori(1, NT // 2) as p:
                for i in range(2):
                    turned_high(2 * p + i, i)

            turn_ln(2)
            for g in range(TG):
                ln_high(2, g)
            moe(1)

        @block.tensor
        def _(pe):
            def mm3(dst, lh, ll, rh, rl, start=True, stop=True, inc=None):
                pe.matmul(dst, lh, rh, start=start, stop=False, skip_group_check=True)
                pe.matmul(dst, lh, rl, start=False, stop=False, skip_group_check=True)
                last = pe.matmul(dst, ll, rh, start=False, stop=stop, skip_group_check=True)
                if inc is not None:
                    last.then_inc(inc, 1)

            def turn_ln(n):
                for g in range(TG):
                    pe.wait_ge(xn_ready, TG * n + g + 1)
                    if g >= 2 or n > 0:
                        pe.wait_ge(xl_ready, TG * n + g - 1)
                    for t in range(TPG):
                        c = (g * TPG + t) * D
                        last = pe.transpose(bank[6 + g % 2][:, t * P:(t + 1) * P], xn[:, c:c + D], ident[:, :])
                    last.then_inc(xn_turned, 1)

            pe.wait_ge(ident_ready, 1)
            pe.wait_ge(rows_in, 16 * 6)
            pe.transpose(bank[5][:, 0:E * FB], rows[:, :], ident[0:E * FB, 0:E * FB])
            pe.transpose(bank[5][:, 96:96 + PAIRS], vrows, ident[0:PAIRS, 0:PAIRS])
            pe.transpose(bank[5][:, 32:32 + H], qkrows[:, 0, :], ident[0:H, 0:H])
            pe.transpose(bank[5][:, 64:64 + H], qkrows[:, 1, :], ident[0:H, 0:H]).then_inc(bias_turned, 1)
            turn_ln(0)

            def moe(k):
                base = k * UNITS
                if k == 0:
                    pe.wait_ge(gl_ready, 1)
                    pe.wait_ge(bias_ready, 6)
                pe.wait_ge(xl_ready, TG * (2 * k + 1))
                for n in range(NT):
                    t = slice(n * P, (n + 1) * P)
                    dst = bank[5][:, n * E:(n + 1) * E]
                    for a, (lhs, rhs) in enumerate(((xh, gh), (xh, gl), (xl, gh), (xl, gl))):
                        last = pe.matmul(dst, lhs[:, t], rhs[:, :], start=(n == 0 and a == 0), stop=(a == 3),
                                         skip_group_check=True)
                last.then_inc(logit_done, 1)
                if k == 0:
                    pe.wait_ge(w1h_ready, 4)
                    pe.wait_ge(w1l_ready, 4)

                def hidden(p, q, e, tg):
                    n = base + 2 * p + q
                    for f in range(FB):
                        wait(pe, gelu_done, FB * (n - 1) + f + 1)
                        c = ds(e * F + f * P, P)
                        t = ds(tg * TGW, TGW)
                        mm3(bank[f][:, :], w1h[:, c], w1l[:, c], xh[:, t], xl[:, t], inc=hid_done)

                def down(p, q, e):
                    n = base + 2 * p + q
                    wait(pe, y_added, n - 1)
                    if k == 0:
                        wait(pe, comb_ready, 1 if isinstance(p, int) and p == 0 else 0)
                    for f in range(FB):
                        pe.wait_ge(hl_done, FB * n + f + 1)
                        c = ds((e * FB + f) * D, D)
                        for t in range(TPG):
                            b = slice(t * P, (t + 1) * P)
                            mm3(bank[4 + q][:, b], hh[q][f][:, b], hl[q][f][:, b], w2h[:, c], w2l[:, c],
                                start=(f == 0 and t == 0), stop=(f == FB - 1),
                                inc=y_done if (f, t) == (FB - 1, TPG - 1) else None)

                def at(v):
                    if isinstance(v, int):
                        return v % E, v // E
                    return pe.snap(v % E), pe.snap(v // E)

                hidden(0, 0, *at(0))

                def pair(p, last=False):
                    e0, _ = at(2 * p)
                    e1, t1 = at(2 * p + 1)
                    hidden(p, 1, e1, t1)
                    down(p, 0, e0)
                    if not last:
                        e2, t2 = at(2 * p + 2)
                        hidden(p + 1, 0, e2, t2)
                    down(p, 1, e1)

                if k == 0:
                    pe.wait_ge(w2h_ready, 4)
                    pe.wait_ge(w2l_ready, 4)
                pair(0)
                with pe.Fori(1, UNITS // 2 - 1) as p:
                    pair(p)
                pe.wait_ge(comb_ready, k + 1)
                pe.transpose(bank[6][:, 0:P], comb[:, :, :].rearrange("p n e -> p (n e)"), ident[:, :]).then_inc(comb_turned, 1)
                pe.wait_ge(combT_ready, k + 1)
                pe.wait_ge(b2_in, 16 * NT * (k + 1))
                for g in range(TG):
                    if g >= 1:
                        wait(pe, b2_added, TG * k + g - 1)
                    pe.matmul(bank[6 + (g + 1) % 2][:, :], combT[:, :], b2diag[:, g * TGW:(g + 1) * TGW],
                              start=True, stop=True).then_inc(b2_done, 1)
                pair(UNITS // 2 - 1, last=True)

            moe(0)

            turn_ln(1)
            pe.wait_ge(al_ready, 1)
            for c in range(PAIRS):
                vh, vl = (t[:, c:c + 1].to_broadcast([P, P]) for t in (vbias_h, vbias_l))
                b = slice(c * D, (c + 1) * D)
                mm3(bank[5][:, 0:D], vh, vl, fo_h[:, b], fo_l[:, b], start=(c == 0), stop=(c == PAIRS - 1),
                    inc=vbias_done if c == PAIRS - 1 else None)
            for i in range(3 * TG):
                g, w = divmod(i, 3)
                t = slice(g * TGW, (g + 1) * TGW)
                pe.wait_ge(xl_ready, TG + g + 1)
                if i == 5:
                    pe.wait_ge(obias_ready, 1)
                wait(pe, ul_ready, i - 5)
                wh, wl = (m[:, w, :, :].rearrange("p r d -> p (r d)") for m in (pwh, pwl))
                mm3(bank[i % 6][:, :], wh, wl, xh[:, t], xl[:, t], inc=u_done)

            def fill(x_, i, f, b):
                kind, n = FILLS[f]
                dst = extra(f)
                g = f - 3 if f >= 3 else max(n for n in range(len(FILLS)) if n % 3 == f)
                y = x_ if f >= 3 else x_ - 1
                pk, pn = FILLS[g]
                if pk in "qk":
                    s, v = qk_lo, 4 * y + QK.index(g) + 1
                elif pk == "v":
                    s, v = v_lo, y + 1
                elif pk == "m":
                    s, v = smax_red, STEPS * y + pn + 1
                else:
                    s, v = mrow_ready, 2 * y + pn + 1
                wait(pe, s, v)
                if kind in "qkv":
                    hx = column(pe, x_, b)
                if kind in "qk":
                    w = "qk".index(kind)
                    uu = u[w][:, b * SEQ + n * TGW:b * SEQ + (n + 1) * TGW]
                    fh, fl = (m[:, w, :, :, :].rearrange("p h r d -> p (h r d)")[:, ds(hx * P, P)]
                              for m in (fqk_h, fqk_l))
                    pe.matmul(dst[:, :], fh, uu, start=True, stop=False)
                    pe.matmul(dst[:, :], fl, uu, start=False, stop=True).then_inc(qk_done, 1)
                elif kind == "v":
                    c = ds(hx * DK, DK)
                    for j in range(JB):
                        uu = u[2][:, b * SEQ + j * P:b * SEQ + (j + 1) * P]
                        pe.matmul(dst[:, j * DK:(j + 1) * DK], uu, fv_h[:, c], start=(j == 0), stop=False,
                                  skip_group_check=True)
                        last = pe.matmul(dst[:, j * DK:(j + 1) * DK], uu, fv_l[:, c], start=False, stop=True,
                                         skip_group_check=True)
                    last.then_inc(v_done, 1)
                elif kind == "m":
                    ib, half = divmod(n, 2)
                    if n < 2:
                        pe.wait_ge(qk_hi, 4 * x_ + 2 * n + 2)
                        pe.wait_ge(qk_lo, 4 * x_ + 1)
                    if n == STEPS // 2:
                        pe.wait_ge(qk_lo, 4 * x_ + 3)
                    pe.matmul(dst[:, :], q1[i][:, ib * P:(ib + 1) * P], k1[i][:, half * TGW:(half + 1) * TGW],
                              start=True, stop=True).then_inc(smax_done, 1)
                else:
                    if n == 0:
                        pe.wait_ge(negmax_ready, x_ + 1)
                    for t in range(TPG):
                        col = negmax[i][:, n * TPG + t:n * TPG + t + 1].to_broadcast([P, P])
                        last = pe.matmul(dst[:, t * P:(t + 1) * P], col, ident16[:, :], start=(t == 0), stop=True,
                                         skip_group_check=True)
                    last.then_inc(mrow_done, 1)

            def scores(h, i, s):
                j, half = divmod(s, 2)
                if s == 0:
                    pe.wait_ge(qk_lo, 4 * h + 4)
                    pe.wait_ge(q2_hi, 2 * h + 2)
                    pe.wait_ge(mrow_ready, 2 * h + 2)
                wait(pe, exp_done, STEPS * h + s - 1)
                c, t = slice(j * P, (j + 1) * P), slice(half * TGW, (half + 1) * TGW)
                pe.matmul(bank[3 + s % 2][:, :], k1[i][:, c], q1[i][:, t], start=True, stop=False)
                pe.matmul(bank[3 + s % 2][:, :], k2[i][:, c], q2[i][:, t], start=False, stop=True).then_inc(st_done, 1)

            def values(h, i, s):
                j, half = divmod(s, 2)
                if s == 0:
                    wait(pe, acc_out, h)
                    pe.wait_ge(v_lo, h + 1)
                pe.wait_ge(*split_count(h, s))
                hi = prob[s % RING].bitcast(BF16).rearrange("p (n t) -> p n t", t=2)[:, :, 1]
                for t in range(TPG):
                    blk = half * TPG + t
                    dst = bank[blk // 3][:, blk % 3 * VW:(blk % 3 + 1) * VW]
                    c = slice(t * P, (t + 1) * P)
                    pe.matmul(dst, hi[:, c], vv[i][:, j, 0:VW], start=(j == 0 and blk % 3 == 0), stop=False,
                              skip_group_check=True)
                    last = pe.matmul(dst[:, 0:DK + 1], plow[s % RING][:, c], vv[i][:, j, 0:DK + 1], start=False,
                                     stop=(j == JB - 1), skip_group_check=True)
                last.then_inc(pv_done, 1)

            def head(h, i, b, first=False, last=False):
                for s in range(STEPS):
                    scores(h, i, s)
                    if not last:
                        for f in PE_FILLS[s][0]:
                            fill(h + 1, 1 - i, f, b)
                    for t in PV_AT[s]:
                        if t >= 0:
                            values(h, i, t)
                        elif not first:
                            values(h - 1, 1 - i, t + STEPS)
                    if not last:
                        for f in PE_FILLS[s][1]:
                            fill(h + 1, 1 - i, f, b)

            pe.wait_ge(ul_ready, 3 * TG)
            pe.wait_ge(pad_ready, 2)
            for f in range(len(FILLS)):
                fill(0, 0, f, 0)
            run_heads(pe, head)
            for t in range(STEPS - 6, STEPS):
                values(NH - 1, 1, t)

            def turn_heads(n, i):
                wait(pe, ol_ready, 2 * n - 2)
                for c in range(2):
                    for t in range(TPG):
                        src = heads[:, :, :].rearrange("p n d -> p (n d)")[
                            :, ds(n * H * DK + (c * TPG + t) * P, P)]
                        last = pe.transpose(bank[2 * i + c][:, t * P:(t + 1) * P], src, ident[:, :])
                    last.then_inc(o_turned, 1)

            def project(n, i):
                wait(pe, o_added, n - 1)
                pe.wait_ge(ol_ready, 2 * n + 2)
                for c in range(PAIRS):
                    b = slice(c * P, (c + 1) * P)
                    mm3(bank[4 + i][:, 0:D], oh[i][:, b], ol[i][:, b], fo_h[:, b], fo_l[:, b], start=(c == 0),
                        stop=(c == PAIRS - 1), inc=o_done if c == PAIRS - 1 else None)

            def out_pair(p, last=False):
                turn_heads(2 * p + 1, 1)
                project(2 * p, 0)
                if not last:
                    turn_heads(2 * p + 2, 0)
                project(2 * p + 1, 1)

            pe.wait_ge(head_ready, NH)
            turn_heads(0, 0)
            for p in range(NT // 2):
                out_pair(p, last=p == NT // 2 - 1)

            turn_ln(2)
            moe(1)

        @block.vector
        def _(dve):
            steps = [0]

            def then(ins):
                steps[0] += 1
                ins.then_inc(dve_step, 1)
                dve.wait_ge(dve_step, steps[0])

            def layer_norm(n):
                for t in range(NT):
                    if n == 0 and t % TPG == 0:
                        dve.wait_ge(x_in[t // TPG], 16)
                    last = dve.bn_stats(stats[:, t, :], x[:, t * D:(t + 1) * D])
                then(last)
                for t in range(NT):
                    last = dve.bn_aggr(mv[:, t, :], stats[:, t, :])
                then(last)
                dve.tensor_scalar(var_eps[:, :], mv[:, :, 1], EPS, None, ALU.add).then_inc(var_ready, 1)
                dve.wait_ge(sd_ready, n + 1)
                then(dve.reciprocal(rstd[:, :], sd[:, :]))
                for g in range(TG):
                    if n > 0 and g == 0:
                        dve.wait_ge(xn_turned, TG * n)
                    for t in range(g * TPG, (g + 1) * TPG):
                        last = dve.tensor_scalar(xn[:, t * D:(t + 1) * D], x[:, t * D:(t + 1) * D], mv[:, t, 0:1],
                                                 rstd[:, t:t + 1], ALU.subtract, ALU.mult)
                    last.then_inc(xn_ready, 1)
                for g in range(TG):
                    s = slice(g * TGW, (g + 1) * TGW)
                    dve.wait_ge(xh_ready, TG * n + g + 1)
                    dve.tensor_tensor(xl[:, s], bank[6 + g % 2], xh[:, s], ALU.subtract).then_inc(xl_ready, 1)
                    if n == 0:
                        c = slice(g * 1024, (g + 1) * 1024)
                        dve.wait_ge(w1h_ready, g + 1)
                        dve.tensor_tensor(w1l[:, c], w1_32[:, c], w1h[:, c], ALU.subtract).then_inc(w1l_ready, 1)

            layer_norm(0)
            dve.wait_ge(gh_ready, 1)
            dve.tensor_tensor(gl[:, :], gate32[:, :], gh[:, :], ALU.subtract).then_inc(gl_ready, 1)
            dve.wait_ge(bias_turned, 1)
            dve.tensor_copy(b1c[:, :], bank[5][:, 0:E * FB]).then_inc(bias_ready, 1)
            dve.tensor_copy(vbias[:, :], bank[5][:, 96:96 + PAIRS]).then_inc(bias_ready, 1)
            dve.tensor_copy(vbias_h[:, :], bank[5][:, 96:96 + PAIRS]).then_inc(bias_ready, 1)
            dve.wait_ge(bias_ready, 3)
            dve.tensor_tensor(vbias_l[:, :], vbias[:, :], vbias_h[:, :], ALU.subtract).then_inc(bias_ready, 1)
            dve.tensor_copy(qkbias[:, :, 0], bank[5][:, 32:32 + H]).then_inc(bias_ready, 1)
            dve.tensor_copy(qkbias[:, :, 1], bank[5][:, 64:64 + H]).then_inc(bias_ready, 1)
            for c in range(4):
                s = slice(c * 1024, (c + 1) * 1024)
                dve.wait_ge(w2_in[c], 16)
                dve.tensor_copy(w2h[:, s], w2_32[:, s]).then_inc(w2h_ready, 1)

            def router(k):
                dve.wait_ge(logit_done, k + 1)
                then(dve.tensor_copy(logit[:, :, :].rearrange("p n e -> p (n e)"), bank[5][:, 0:NT * E]))
                mine = logit[:, :, :].unsqueeze(3).to_broadcast([P, NT, E, E])
                other = logit[:, :, :].unsqueeze(2).to_broadcast([P, NT, E, E])
                above = xn[:, 0:NT * E * E].rearrange("p (n e o) -> p n e o", e=E, o=E)
                equal = xn[:, NT * E * E:2 * NT * E * E].rearrange("p (n e o) -> p n e o", e=E, o=E)
                dve.wait_ge(before_ready, 1)
                dve.tensor_tensor(above, other, mine, ALU.is_gt)
                then(dve.tensor_tensor(equal, other, mine, ALU.is_equal))
                then(dve.tensor_tensor(equal, equal, before[:, :, :].unsqueeze(1).to_broadcast([P, NT, E, E]), ALU.mult))
                then(dve.tensor_tensor(above, above, equal, ALU.add))
                then(dve.tensor_reduce(rank[:, :, :], above, AX.X, ALU.add))
                for r in range(2):
                    then(dve.tensor_scalar(sel[:, r, :, :], rank[:, :, :], float(r), None, ALU.is_equal))
                    then(dve.tensor_tensor(picked[:, :, :], sel[:, r, :, :], logit[:, :, :], ALU.mult))
                    then(dve.tensor_reduce(top[:, r, :], picked[:, :, :], AX.X, ALU.add))
                dve.tensor_tensor(gap[:, :], top[:, 1, :], top[:, 0, :], ALU.subtract).then_inc(gap_ready, 1)
                dve.wait_ge(expgap_ready, k + 1)
                then(dve.tensor_scalar(wtop[:, 0, :], expgap[:, :], 1.0, None, ALU.add))
                then(dve.reciprocal(wtop[:, 1, :], wtop[:, 0, :]))
                then(dve.tensor_tensor(wtop[:, 2, :], wtop[:, 1, :], expgap[:, :], ALU.mult))
                for r in range(2):
                    then(dve.tensor_tensor(sel[:, r, :, :], sel[:, r, :, :],
                                           wtop[:, 1 + r, :].unsqueeze(2).to_broadcast([P, NT, E]), ALU.mult))
                then(dve.tensor_tensor(picked[:, :, :], sel[:, 0, :, :], sel[:, 1, :, :], ALU.add))
                dve.tensor_scalar(comb[:, :, :], picked[:, :, :], 0.5, None, ALU.mult).then_inc(comb_ready, 1)
                dve.wait_ge(comb_ready, k + 1)

            def moe(k):
                base = k * UNITS
                router(k)

                def at(v):
                    if isinstance(v, int):
                        return v % E, v // E
                    return dve.snap(v % E), dve.snap(v // E)

                def high(p, q):
                    n = base + 2 * p + q
                    for f in range(FB):
                        dve.wait_ge(gelu_done, FB * n + f + 1)
                        if f == 0:
                            wait(dve, y_done, n - 1)
                        dve.tensor_copy(hh[q][f], g32[q][f]).then_inc(hh_done, 1)

                def add(v, q):
                    e, tg = at(v)
                    dve.wait_ge(y_done, base + v + 1)
                    wait(dve, y_added, base + v)
                    for t in range(TPG):
                        xs = x[:, ds((tg * TPG + t) * D, D)]
                        w = comb[:, :, :].rearrange("p n e -> p (n e)")[:, ds((tg * TPG + t) * E + e, 1)]
                        last = dve.scalar_tensor_tensor(out=xs, in0=bank[4 + q][:, t * P:(t + 1) * P], scalar=w,
                                                        in1=xs, op0=ALU.mult, op1=ALU.add)
                    last.then_inc(y_added, 1)

                def pair(p, first=False):
                    high(p, 0)
                    if not first:
                        add(2 * p - 1, 1)
                    high(p, 1)
                    add(2 * p, 0)

                pair(0, first=True)
                with dve.Fori(1, UNITS // 2 - 1) as p:
                    pair(p)
                dve.wait_ge(comb_turned, k + 1)
                dve.tensor_copy(combT[:, :], bank[6][:, 0:P]).then_inc(combT_ready, 1)
                dve.wait_ge(y_added, base + UNITS - 3)
                for g in range(TG):
                    s = slice(g * TGW, (g + 1) * TGW)
                    dve.wait_ge(b2_done, TG * k + g + 1)
                    last = dve.tensor_tensor(x[:, s], x[:, s], bank[6 + (g + 1) % 2], ALU.add)
                    last.then_inc(b2_added, 1)
                dve.wait_ge(b2_added, TG * (k + 1))
                pair(UNITS // 2 - 1)
                add(UNITS - 1, 1)
                dve.wait_ge(y_added, base + UNITS)

            moe(0)
            layer_norm(1)
            dve.wait_ge(obias_in, 16)
            dve.wait_ge(vbias_done, 1)
            dve.tensor_tensor(obias[:, :], bank[5][:, 0:D], obias[:, :], ALU.add).then_inc(obias_ready, 1)
            for i in range(3 * TG):
                g, w = divmod(i, 3)
                s = slice(g * TGW, (g + 1) * TGW)
                dve.wait_ge(uh_ready, i + 1)
                dve.tensor_tensor(u[w][DK:P, s], bank[i % 6][DK:P, :], u[w][DK:P, s], ALU.subtract).then_inc(ul_ready, 1)

            def fill(x_, i, f, b):
                kind, n = FILLS[f]
                half = slice(n * TGW, (n + 1) * TGW)
                if kind in "qk":
                    dve.wait_ge(qk_hi, 4 * x_ + QK.index(f) + 1)
                    if kind == "q":
                        dve.wait_ge(q2_hi, 2 * x_ + n + 1)
                    if kind == "q":
                        dve.scalar_tensor_tensor(out=q1[i][DK:P, half], in0=extra(f)[DK:P, :],
                                                 scalar=hbias[i][DK:P, 0:1], in1=q1[i][DK:P, half],
                                                 op0=ALU.add, op1=ALU.subtract).then_inc(qk_lo, 1)
                    else:
                        dve.scalar_tensor_tensor(out=k2[i][0:DK, half], in0=extra(f)[0:DK, :],
                                                 scalar=hbias[i][0:DK, 1:2], in1=k1[i][0:DK, half],
                                                 op0=ALU.add, op1=ALU.subtract).then_inc(qk_lo, 1)
                elif kind == "v":
                    dve.wait_ge(v_hi, x_ + 1)
                    dve.tensor_tensor(vv[i][:, :, DK + 1:VW], extra(f).rearrange("p (j d) -> p j d", d=DK),
                                      vv[i][:, :, 0:DK], ALU.subtract).then_inc(v_lo, 1)
                elif kind == "m":
                    dve.wait_ge(smax_done, STEPS * x_ + n + 1)
                    dve.tensor_reduce(tilemax[i][:, n:n + 1], extra(f)[:, :], AX.X, ALU.max).then_inc(smax_red, 1)
                    if n == STEPS - 1:
                        dve.wait_ge(smax_red, STEPS * (x_ + 1))
                        wait(dve, mrow_done, 2 * x_ - 2)
                        dve.tensor_reduce(negmax[i][:, :], tilemax[i][:, :].rearrange("p (b h) -> p b h", h=2),
                                          AX.X, ALU.max, negate=True).then_inc(negmax_ready, 1)

            def normalise(h):
                if isinstance(h, int):
                    hx, bx = h % H, h // H
                else:
                    hx, bx = dve.snap(h % H), dve.snap(h // H)
                dve.wait_ge(acc_out, h + 1)
                dve.reciprocal(rsum[:, :], acc_sb[:, :, DK]).then_inc(norm_step, 1)
                dve.wait_ge(norm_step, h + 1)
                dve.wait_ge(acc_sum, h + 1)
                dst = heads[:, ds(bx * JB, JB), ds(hx * DK, DK)]
                dve.tensor_tensor(dst, acc_sb[:, :, 0:DK], rsum[:, :].unsqueeze(2).to_broadcast([P, JB, DK]),
                                  ALU.mult).then_inc(head_ready, 1)

            def head(h, i, b, first=False, last=False):
                for s in range(STEPS):
                    if s == NORM_STEP and not first:
                        normalise(h - 1)
                    if s in DVE_SPLITS:
                        dve.wait_ge(exp_done, STEPS * h + s + 1)
                        hi = prob[s % RING].bitcast(BF16).rearrange("p (n t) -> p n t", t=2)[:, :, 1]
                        dve.tensor_tensor(plow[s % RING], prob[s % RING], hi, ALU.subtract).then_inc(plow_dve, 1)
                    if not last:
                        for f in DVE_FILLS[s]:
                            fill(h + 1, 1 - i, f, b)

            for f in range(len(FILLS)):
                fill(0, 0, f, 0)
            run_heads(dve, head)
            normalise(NH - 1)

            def turned_low(n, i):
                for c in range(2):
                    b = slice(c * TGW, (c + 1) * TGW)
                    dve.wait_ge(oh_ready, 2 * n + c + 1)
                    dve.tensor_tensor(ol[i][:, b], bank[2 * i + c][:, :], oh[i][:, b], ALU.subtract).then_inc(ol_ready, 1)

            def add_out(n, i):
                dve.wait_ge(o_done, n + 1)
                xs = x[:, ds(n * D, D)]
                dve.tensor_tensor(xs, xs, bank[4 + i][:, 0:D], ALU.add).then_inc(o_added, 1)

            def out_pair(p, first=False):
                turned_low(2 * p, 0)
                if not first:
                    add_out(2 * p - 1, 1)
                turned_low(2 * p + 1, 1)
                add_out(2 * p, 0)

            dve.wait_ge(xbias_added, 1)
            out_pair(0, first=True)
            with dve.Fori(1, NT // 2) as p:
                out_pair(p)
            add_out(NT - 1, 1)
            dve.wait_ge(o_added, NT)
            layer_norm(2)
            moe(1)


_INS = ["attn_z", "attn_wq", "attn_wk", "attn_wv", "attn_fcq_w", "attn_fcq_b", "attn_fck_w", "attn_fck_b",
        "attn_fcv_w", "attn_fcv_b", "attn_fco_w", "attn_fco_b", "ffn_gate_w", "ffn_w1", "ffn_b1", "ffn_w2", "ffn_b2"]


def kernel(**inputs):
    import numpy as np
    import concourse.bacc as bacc
    from concourse.bass_utils import run_bass_kernel_spmd

    nc = bacc.Bacc("TRN2", target_bir_lowering=False, num_devices=1)
    arrays, args = {}, []
    for name in _INS:
        a = np.ascontiguousarray(inputs[f"L0_{name}"])
        arrays[name] = a
        args.append(nc.dram_tensor(name, a.shape, mybir.dt.from_np(a.dtype), kind="ExternalInput").ap())
    y = nc.dram_tensor("y", arrays["attn_z"].shape, F32, kind="ExternalOutput").ap()
    macaron_block(nc, *args, y)
    result = run_bass_kernel_spmd(nc, [arrays], core_ids=[0])
    return result.results[0]["y"]
```

```python
from contextlib import ExitStack

import concourse.bass as bass
from concourse import mybir

F32 = mybir.dt.float32
F16 = mybir.dt.float16
BF16 = mybir.dt.bfloat16
ACT = mybir.ActivationFunctionType
ALU = mybir.AluOpType
AX = mybir.AxisListType
ds = bass.ds


def macaron_block(nc, z, wq, wk, wv, fcq_w, fcq_b, fck_w, fck_b, fcv_w, fcv_b, fco_w, fco_b,
                  gate_w, w1, b1, w2, b2, out):
    P = 128
    BATCH, SEQ, D = z.shape
    T = BATCH * SEQ
    NT = T // P
    TGW = 512
    TG = T // TGW
    TPG = TGW // P
    E, _, F = w1.shape
    FB = F // P
    DK = wq.shape[1]
    H = fcq_w.shape[1] // DK
    NH = BATCH * H
    JB = SEQ // P
    HALVES = SEQ // TGW
    STEPS = JB * HALVES
    VW = 2 * DK + 1
    PAIRS = H * DK // P
    UNITS = TG * E
    HEAD_PAIRS = (4, 1)
    TAIL = 12
    LATE = (2, 3), (3,)
    EPS = 1e-5
    SCALE = float(DK) ** -0.5
    assert (D, DK, F, JB, STEPS) == (128, 64, 512, 8, 16)

    z_t = z.rearrange("b (n p) d -> p (b n) d", p=P)
    out_t = out.rearrange("b (n p) d -> p (b n) d", p=P)

    with ExitStack() as ctx:
        def sb(name, shape, dt):
            return ctx.enter_context(nc.sbuf_tensor(name, shape, dt))

        def sem(name):
            return ctx.enter_context(nc.semaphore(name))

        bank = [ctx.enter_context(nc.psum_tensor(f"bank{i}", [P, 512], F32))[:, :] for i in range(8)]

        x = sb("x", [P, NT * D], F32)
        xh = sb("xh", [P, T], F16)
        xl = sb("xl", [P, T], F16)
        w1h = sb("w1h", [P, E * F], F16)
        w1l = sb("w1l", [P, E * F], F16)
        w2h = sb("w2h", [P, E * FB * D], F16)
        w2l = sb("w2l", [P, E * FB * D], F16)
        b1c = sb("b1c", [P, E * FB], F32)
        gh = sb("gh", [P, E], F16)
        gl = sb("gl", [P, E], F16)
        gate32 = sb("gate32", [P, E], F32)
        ident = sb("ident", [P, P], F32)
        ident16 = sb("ident16", [P, P], F16)
        minus_ident16 = sb("minus_ident16", [P, P], F16)
        falling = sb("falling", [P, E], F32)
        qkbias = sb("qkbias", [P, H, 2], F32)
        hbias = [sb(f"hbias{i}", [P, 2], F32) for i in range(2)]
        vbias = sb("vbias", [P, PAIRS], F32)
        vbias_h = sb("vbias_h", [P, PAIRS], F16)
        vbias_l = sb("vbias_l", [P, PAIRS], F16)
        obias = sb("obias", [P, D], F32)
        pw32 = sb("pw32", [P, 3, DK], F32)
        pwh = sb("pwh", [P, 3, 2, DK], F16)
        pwl = sb("pwl", [P, 3, 2, DK], F16)
        fqk_h = sb("fqk_h", [P, 2, H, 2, DK], F16)
        fqk_l = sb("fqk_l", [P, 2, H, 2, DK], F16)
        fv_h = sb("fv_h", [P, H * DK], F16)
        fv_l = sb("fv_l", [P, H * DK], F16)
        fo_h = sb("fo_h", [P, PAIRS * D], F16)
        fo_l = sb("fo_l", [P, PAIRS * D], F16)
        u = [sb(f"u{n}", [P, T], F16) for n in "qkv"]

        stats = sb("stats", [P, NT, 6], F32)
        mv = sb("mv", [P, NT, 2], F32)
        var_eps = sb("var_eps", [P, NT], F32)
        sd = sb("sd", [P, NT], F32)
        rstd = sb("rstd", [P, NT], F32)
        logit = sb("logit", [P, NT, E], F32)
        masked = sb("masked", [P, NT, E], F32)
        is_top = sb("is_top", [P, NT, E], F32)
        first = sb("first", [P, NT], F32)
        sel = sb("sel", [P, 2, NT, E], F32)
        picked = sb("picked", [P, NT, E], F32)
        top = sb("top", [P, 2, NT], F32)
        gap = sb("gap", [P, NT], F32)
        expgap = sb("expgap", [P, NT], F32)
        wtop = sb("wtop", [P, 3, NT], F32)
        comb = sb("comb", [P, NT, E], F32)
        combT = sb("combT", [P, P], F32)

        heads = sb("heads", [P, NT, H * DK], F32)
        stage = heads[:, :, :].rearrange("p n d -> p (n d)")
        w1_32 = stage[:, 0:E * F]
        b2diag = stage[:, 0:NT * D]
        w2_32 = stage[:, E * F:2 * E * F]
        fqk_32 = stage[:, 2 * E * F:2 * E * F + 2 * H * DK].rearrange("p (w h d) -> p w h d", w=2, h=H)
        fv_32 = stage[:, 2 * E * F + 2 * H * DK:2 * E * F + 3 * H * DK]
        fo_32 = stage[:, 2 * E * F + 3 * H * DK:2 * E * F + 4 * H * DK]

        work = sb("work", [P, 8256], F32)

        def view(a, n, dt=F32):
            v = work[:, a:a + n]
            return v if dt == F32 else v.bitcast(dt)

        g32 = [[view((2 * q + 0) * 1024 + 512 * f if f < 2 else (2 * q + 1) * 1024 + 512 * (f - 2), 512)
                for f in range(FB)] for q in range(2)]
        hh = [[view(4096 + 1024 * q + 256 * f, 256, F16) for f in range(FB)] for q in range(2)]
        hl = [[view(6144 + 1024 * q + 256 * f, 256, F16) for f in range(FB)] for q in range(2)]

        XN = [stage[:, 6 * NT * D:7 * NT * D]] * 2 + [stage[:, NT * D:2 * NT * D]]
        rows = work[0:E * FB, 0:P]
        vrows = work[0:PAIRS, 3 * P:4 * P]
        qkrows = work[0:H, P:3 * P].rearrange("p (w c) -> p w c", w=2)

        q1 = [view(2048 * i, 512, F16) for i in range(2)]
        q2 = [view(2048 * i + 512, 512, F16) for i in range(2)]
        k1 = [view(2048 * i + 1024, 512, F16) for i in range(2)]
        k2 = [view(2048 * i + 1536, 512, F16) for i in range(2)]
        VPITCH = 132
        vv = [view(4096 + i * JB * VPITCH // 2, JB * VPITCH // 2, F16)
              .rearrange("p (j c) -> p j c", j=JB) for i in range(2)]
        prob = [view(5184 + 512 * i, 512) for i in range(4)]
        prob += [t[:, TGW * 2 * i:TGW * 2 * (i + 1)].bitcast(F32) for t in (xh, xl) for i in range(2)]
        plow = [view(7232 + 256 * i, 256, F16) for i in range(4)]
        plow += [sb(f"plow{i}", [P, TGW], F16)[:, :] for i in range(4)]
        RING = len(prob)
        acc_sb = sb("acc_sb", [P, JB, VW], F32)
        rsum = sb("rsum", [P, JB], F32)
        tilemax = [sb(f"tilemax{i}", [P, STEPS], F32) for i in range(2)]
        negmax = [sb(f"negmax{i}", [P, DK + JB], F16) for i in range(2)]
        maxrows = [sb(f"maxrows{i}", [P, P], F16) for i in range(2)]
        tilemask = sb("tilemask", [P, JB, P], F16)
        oh = [view(1024 * i, 512, F16) for i in range(2)]
        ol = [view(1024 * i + 512, 512, F16) for i in range(2)]

        x_in = [sem(f"x_in{i}") for i in range(TG)]
        w1_in = [sem(f"w1_in{i}") for i in range(4)]
        w2_in = [sem(f"w2_in{i}") for i in range(4)]
        gate_in, rows_in, b2_in, attn_in, obias_in = (sem(n) for n in ("gate_in", "rows_in", "b2_in", "attn_in", "obias_in"))
        ident_ready, falling_ready, b2_zeroed, pad_ready = (sem(n) for n in ("ident_ready", "falling_ready", "b2_zeroed", "pad_ready"))
        w1h_ready, w1l_ready, w2h_ready, w2l_ready = (sem(n) for n in ("w1h_ready", "w1l_ready", "w2h_ready", "w2l_ready"))
        gh_ready, gl_ready, ah_ready, al_ready = (sem(n) for n in ("gh_ready", "gl_ready", "ah_ready", "al_ready"))
        bias_turned, bias_ready = sem("bias_turned"), sem("bias_ready")
        stats_ready, var_ready, sd_ready, rstd_ready, xn_ready, xn_pool, xn_turned, xh_ready, xl_ready = (
            sem(n) for n in ("stats_ready", "var_ready", "sd_ready", "rstd_ready", "xn_ready", "xn_pool", "xn_turned",
                             "xh_ready", "xl_ready"))
        logit_done, logit_read, gap_ready, expgap_ready, comb_ready, comb_turned, combT_ready, b2_done, b2_added = (
            sem(n) for n in ("logit_done", "logit_read", "gap_ready", "expgap_ready", "comb_ready", "comb_turned", "combT_ready", "b2_done", "b2_added"))
        hid_done, gelu_done, hh_done, hl_done, y_done, y_added = (
            sem(n) for n in ("hid_done", "gelu_done", "hh_done", "hl_done", "y_done", "y_added"))
        u_done, uh_ready, ul_ready = (sem(n) for n in ("u_done", "uh_ready", "ul_ready"))
        qk_done, qk_hi, qk_lo, q2_hi, v_done, v_hi, v_lo = (
            sem(n) for n in ("qk_done", "qk_hi", "qk_lo", "q2_hi", "v_done", "v_hi", "v_lo"))
        smax_done, smax_red, negmax_ready, maxrows_done, maxrows_ready, mrow_ready = (
            sem(n) for n in ("smax_done", "smax_red", "negmax_ready", "maxrows_done", "maxrows_ready", "mrow_ready"))
        st_done, exp_done, plow_pool, plow_dve, pv_done, acc_out, head_ready = (
            sem(n) for n in ("st_done", "exp_done", "plow_pool", "plow_dve", "pv_done", "acc_out", "head_ready"))
        o_turned, oh_ready, ol_ready, o_done, o_added, xbias_added = (
            sem(n) for n in ("o_turned", "oh_ready", "ol_ready", "o_done", "o_added", "xbias_added"))
        u_rest, ul_act, mask_ready = sem("u_rest"), sem("ul_act"), sem("mask_ready")
        vbias_done, obias_ready, acc_sum = sem("vbias_done"), sem("obias_ready"), sem("acc_sum")
        norm_step, hbias_ready = sem("norm_step"), sem("hbias_ready")
        dve_step, pool_step, stored = sem("dve_step"), sem("pool_step"), sem("stored")

        def wait(eng, s, v):
            if not (isinstance(v, int) and v <= 0):
                eng.wait_ge(s, v)

        FILLS = [("q", 0), ("k", 0), ("q", 1), ("m", 0), ("k", 1), ("m", 1), ("m", 2), ("m", 3),
                 ("m", 4), ("m", 5), ("m", 6), ("m", 7), ("m", 8), ("m", 9), ("m", 10), ("m", 11),
                 ("m", 12), ("m", 13), ("m", 14), ("m", 15), ("r", 0), ("v", 0)]
        PE_FILLS = [([], [0]), ([1, 2], []), ([], []), ([3, 4], [5, 6]), ([7], []), ([8], []),
                    ([9, 10], []), ([], [11]), ([12], [13]), ([14], [15]), ([16], [17]), ([], [18]),
                    ([], [19]), ([], []), ([], [20, 21]), ([], [])]
        ACT_FILLS = [[0], [1, 2, 3], [4], [], [], [], [5, 6], [], [], [7, 8, 9], [],
                     [10, 11, 12, 13, 14, 15, 16, 17, 18], [], [19, 20], [21], []]
        DVE_FILLS = [[0, 1, 2], [3, 4], [5, 6], [], [7, 8], [9, 10], [], [11, 12, 13, 14, 15],
                     [16, 17, 18, 19], [], [], [], [20, 21], [], [], []]
        PV_AT = [[-7], [-6, -5], [-4], [-3, -2, -1], [], [0], [], [], [1], [2, 3], [4], [], [5], [6],
                 [], [7, 8]]
        LATE_VALUES = sum(t < 0 for tiles in PV_AT for t in tiles)
        ACC_STEP, ADD_STEP, NORM_STEP = 4, 5, 13
        DVE_SPLITS = (10, 13, 15)

        QK = [f for f, (kind, _) in enumerate(FILLS) if kind in "qk"]
        assert [FILLS[f] for f in QK] == [("q", 0), ("k", 0), ("q", 1), ("k", 1)]

        STATS_AT, ROOT_AT, TURN_AT = (2, 4, 6), (3, 5, 7), (5, 7)

        POOL_NORMS = ((1, 3), (2, 0), (2, 1))
        DVE_NORMS = [(n, g) for n in range(3) for g in range(TG) if (n, g) not in POOL_NORMS]

        TURN_AFTER = ("m", 6)
        U_AFTER = [("m", i) for i in (8, 10, 12)]
        REST_AFTER = [("m", i) for i in (1, 2, 3, 9, 11, 13)]

        def ln_bank(n, g):
            return bank[4] if (n, g) == (1, TG - 1) else bank[6 + g % 2]

        def u_bank(i):
            return bank[i if i < 6 else (i - 6) % 5]

        def extra(i):
            return bank[5 + i % 3]

        def run_heads(eng, head):
            head(0, 0, 0, first=True)
            head(1, 1, 0)
            for b in range(BATCH):
                with eng.Fori(max(1, b * H // 2), (b + 1) * H // 2 - 1) as p:
                    head(2 * p, 0, b)
                    head(2 * p + 1, 1, b)
                head((b + 1) * H - 2, 0, b)
                head((b + 1) * H - 1, 1, b + 1, last=b == BATCH - 1)

        def column(eng, x_, b):
            return x_ - b * H if isinstance(x_, int) else eng.snap(x_ - b * H)

        def dve_splits(last):
            return tuple(range(1, STEPS, 2)) if last else DVE_SPLITS

        def split_count(h, s):
            mine = dve_splits(isinstance(h, int) and h == NH - 1)
            if s in mine:
                return plow_dve, len(DVE_SPLITS) * h + mine.index(s) + 1
            rest = [t for t in range(STEPS) if t not in mine]
            return plow_pool, (STEPS - len(DVE_SPLITS)) * h + rest.index(s) + 1

        block = ctx.enter_context(nc.Block())

        @block.sync
        def _(sp):
            def load_x(g):
                sp.dma_start(x[:, g * TGW:(g + 1) * TGW].rearrange("p (n d) -> p n d", d=D),
                             z_t[:, g * TPG:(g + 1) * TPG, :]).then_inc(x_in[g], 16)

            def load_w1(c):
                sp.dma_start(w1_32[:, c * 1024:(c + 1) * 1024].rearrange("p (e f) -> p e f", f=F),
                             w1[2 * c:2 * c + 2].rearrange("e d f -> d e f")).then_inc(w1_in[c], 16)

            load_x(0)
            load_w1(0)
            sp.dma_start(gate32[:, :], gate_w).then_inc(gate_in, 16)
            load_x(1)
            sp.dma_start(rows[:, :], b1.rearrange("e (f p) -> (e f) p", p=P)).then_inc(rows_in, 16)
            for w, b in enumerate((fcq_b, fck_b)):
                for r in range(2):
                    sp.dma_start(qkrows[:, w, r * DK:(r + 1) * DK],
                                 b.rearrange("(h d) -> h d", d=DK)).then_inc(rows_in, 16)
            sp.dma_start(vrows, fcv_b.rearrange("(k p) -> k p", p=P)).then_inc(rows_in, 16)
            load_x(2)
            load_x(3)
            for c in range(1, 4):
                load_w1(c)
            for c in range(4):
                sp.dma_start(w2_32[:, c * 1024:(c + 1) * 1024].rearrange("p (e f d) -> p e f d", f=FB, d=D),
                             w2[2 * c:2 * c + 2].rearrange("e (f p) d -> p e f d", p=P)).then_inc(w2_in[c], 16)
            for w, m in enumerate((wq, wk, wv)):
                sp.dma_start(pw32[:, w, :], m).then_inc(attn_in, 16)
            for r in range(2):
                for w, m in enumerate((fcq_w, fck_w)):
                    sp.dma_start(fqk_32[r * DK:(r + 1) * DK, w, :, :],
                                 m.rearrange("k (h d) -> k h d", d=DK)).then_inc(attn_in, 16)
                sp.dma_start(fv_32[r * DK:(r + 1) * DK, :], fcv_w).then_inc(attn_in, 16)
            sp.dma_start(fo_32.rearrange("p (k e) -> p k e", e=D),
                         fco_w.rearrange("(k p) e -> p k e", p=P)).then_inc(attn_in, 16)
            sp.dma_start(obias[:, :], fco_b.rearrange("(a n) -> a n", a=1).partition_broadcast(P)).then_inc(obias_in, 16)
            for k in range(2):
                sp.wait_ge(b2_zeroed, k + 1)
                for n in range(NT):
                    sp.dma_start(b2diag[n * E:(n + 1) * E, n * D:(n + 1) * D], b2).then_inc(b2_in, 16)
            sp.wait_ge(b2_added, 2 * TG)
            sp.wait_ge(y_added, 2 * UNITS - E)
            for g in range(TG):
                if g == TG - 1:
                    sp.wait_ge(y_added, 2 * UNITS)
                sp.dma_start(out_t[:, g * TPG:(g + 1) * TPG, :],
                             x[:, g * TGW:(g + 1) * TGW].rearrange("p (n d) -> p n d", d=D)).then_inc(stored, 16)
            sp.wait_ge(stored, 16 * TG)

        ATTN_DMAS = 3 + 6 + 1

        @block.gpsimd
        def _(pool):
            pool.memset(ident[:, :], 0.0).then_inc(pool_step, 1)
            mask32 = stage[:, 14 * NT * DK:15 * NT * DK].rearrange("p (t c) -> p t c", c=P)
            pool.memset(mask32, 0.0).then_inc(pool_step, 1)
            for e in range(E):
                last = pool.memset(falling[:, e:e + 1], float(E - e))
            last.then_inc(falling_ready, 1)
            pool.wait_ge(pool_step, 2)
            pool.affine_select(out=ident[:, :], in_=ident[:, :], compare_op=ALU.not_equal, fill=1.0, base=0,
                               pattern=[[-1, P]], channel_multiplier=1).then_inc(ident_ready, 1)
            pool.affine_select(out=mask32, in_=mask32, compare_op=ALU.not_equal, fill=1.0, base=-DK,
                               pattern=[[-1, JB], [0, P]], channel_multiplier=1).then_inc(mask_ready, 1)

            def ln_norm(n, g):
                pool.wait_ge(rstd_ready, TG * n + g + 1)
                for t in range(g * TPG, (g + 1) * TPG):
                    last = pool.tensor_scalar(XN[n][:, t * D:(t + 1) * D], x[:, t * D:(t + 1) * D], mv[:, t, 0:1],
                                              rstd[:, t:t + 1], ALU.subtract, ALU.mult)
                last.then_inc(xn_pool, 1)

            def w1_low(c):
                s = slice(c * 1024, (c + 1) * 1024)
                pool.wait_ge(w1h_ready, c + 1)
                pool.tensor_tensor(w1l[:, s], w1_32[:, s], w1h[:, s], ALU.subtract).then_inc(w1l_ready, 1)

            w1_low(0)
            for i in range(2):
                pool.memset(negmax[i][:, 0:DK], 0.0)
            pool.wait_ge(ident_ready, 1)
            pool.wait_ge(mask_ready, 1)
            pool.tensor_copy(tilemask[:, :, :], mask32)
            pool.tensor_copy(ident16[:, :], ident[:, :])
            pool.tensor_scalar(minus_ident16[:, :], ident[:, :], -1.0, None, ALU.mult).then_inc(ident_ready, 1)
            w1_low(1)

            def moe(k):
                base = k * UNITS

                def pair(p):
                    for q in range(2):
                        n = base + 2 * p + q
                        for f in range(FB):
                            pool.wait_ge(hh_done, FB * n + f + 1)
                            pool.tensor_tensor(hl[q][f], g32[q][f], hh[q][f], ALU.subtract).then_inc(hl_done, 1)

                for p in range(HEAD_PAIRS[k]):
                    pair(p)
                    if k == 0 and p < 2:
                        w1_low(p + 2)
                    if p == (2, 0)[k]:
                        pool.wait_ge(*((w1l_ready, 4), (o_turned, 2 * NT))[k])
                        pool.memset(b2diag, 0.0).then_inc(b2_zeroed, 1)
                with pool.Fori(HEAD_PAIRS[k], UNITS // 2) as p:
                    pair(p)

            moe(0)
            pool.wait_ge(y_done, UNITS)
            for i in range(2):
                pool.memset(q2[i][DK:P, :], 0.0)
                last = pool.memset(k2[i][DK:P, :], 1.0)
            last.then_inc(pad_ready, 1)
            pool.wait_ge(pad_ready, 1)
            for i in range(2):
                last = pool.memset(vv[i][:, :, DK:DK + 1], 1.0)
            last.then_inc(pad_ready, 1)
            pool.wait_ge(pad_ready, 2)
            ln_norm(1, TG - 1)

            pool.wait_ge(obias_ready, 1)
            pool.wait_ge(xn_ready, DVE_NORMS.index((1, 2)) + 1)
            pool.wait_ge(xn_pool, 1)
            pool.tensor_tensor(x[:, :].rearrange("p (n d) -> p n d", d=D),
                               x[:, :].rearrange("p (n d) -> p n d", d=D),
                               obias[:, :].unsqueeze(1).to_broadcast([P, NT, D]), ALU.add).then_inc(xbias_added, 1)

            def add_acc(h):
                pool.wait_ge(acc_out, h + 1)
                pool.tensor_tensor(acc_sb[:, :, 0:DK], acc_sb[:, :, 0:DK], acc_sb[:, :, DK + 1:VW],
                                   ALU.add).then_inc(acc_sum, 1)

            def head(h, i, b, first=False, last=False):
                for s in range(STEPS):
                    if s == ADD_STEP and not first:
                        add_acc(h - 1)
                    if s not in dve_splits(last):
                        pool.wait_ge(exp_done, STEPS * h + s + 1)
                        hi = prob[s % RING].bitcast(BF16).rearrange("p (n t) -> p n t", t=2)[:, :, 1]
                        pool.tensor_tensor(plow[s % RING], prob[s % RING], hi, ALU.subtract).then_inc(plow_pool, 1)

            run_heads(pool, head)
            add_acc(NH - 1)
            for g in range(2):
                ln_norm(2, g)
            moe(1)

        @block.scalar
        def _(act):
            def ln_root(n, g):
                t = slice(g * TPG, (g + 1) * TPG)
                act.wait_ge(var_ready, TG * n + g + 1)
                act.activation(sd[:, t], var_eps[:, t], ACT.Sqrt).then_inc(sd_ready, 1)

            def ln_high(n, g):
                act.wait_ge(xn_turned, TG * n + g + 1)
                act.activation(xh[:, g * TGW:(g + 1) * TGW], ln_bank(n, g), ACT.Copy).then_inc(xh_ready, 1)

            def w2_high(c):
                act.wait_ge(w2_in[c], 16)
                s = slice(c * 1024, (c + 1) * 1024)
                act.activation(w2h[:, s], w2_32[:, s], ACT.Copy).then_inc(w2h_ready, 1)

            def attn_high(c):
                act.wait_ge(attn_in, 16 * ATTN_DMAS)
                if c == 0:
                    for r in range(2):
                        act.activation(pwh[:, :, r, :], pw32[:, :, :], ACT.Copy)
                    last = act.activation(fv_h[:, :], fv_32, ACT.Copy)
                elif c < 3:
                    for r in range(2):
                        last = act.activation(fqk_h[:, c - 1, :, r, :], fqk_32[:, c - 1, :, :], ACT.Copy)
                else:
                    last = act.activation(fo_h[:, :], fo_32, ACT.Copy)
                last.then_inc(ah_ready, 1)

            def w1_high(c):
                act.wait_ge(w1_in[c], 16)
                s = slice(c * 1024, (c + 1) * 1024)
                act.activation(w1h[:, s], w1_32[:, s], ACT.Copy).then_inc(w1h_ready, 1)

            ln_root(0, 0)
            act.wait_ge(gate_in, 16)
            act.activation(gh[:, :], gate32[:, :], ACT.Copy).then_inc(gh_ready, 1)
            w1_high(0)
            ln_high(0, 0)
            ln_root(0, 1)
            ln_high(0, 1)
            w1_high(1)
            ln_root(0, 2)
            ln_root(0, 3)

            def moe(k):
                base = k * UNITS

                def gelu(p, q, f):
                    n = base + 2 * p + q
                    e = act.snap((2 * p + q) % E) if not isinstance(p, int) else (2 * p + q) % E
                    act.wait_ge(hid_done, FB * n + f + 1)
                    wait(act, hl_done, FB * (n - 2) + f + 1)
                    c = act.snap(e * FB + f) if not isinstance(e, int) else e * FB + f
                    act.activation(g32[q][f], bank[f], ACT.Gelu, bias=b1c[:, ds(c, 1)]).then_inc(gelu_done, 1)

                def pair(p, aside=None):
                    for q in range(2):
                        for f in range(FB):
                            gelu(p, q, f)
                        if q == 0 and aside is not None:
                            ln_root(1, aside)

                if k == 0:
                    act.wait_ge(bias_ready, 6)
                for f in range(FB):
                    gelu(0, 0, f)
                for g in LATE[k]:
                    ln_high(2 * k, g)
                for f in range(FB):
                    gelu(0, 1, f)
                if k == 0:
                    w2_high(0)
                act.wait_ge(gap_ready, k + 1)
                act.activation(expgap[:, :], gap[:, :], ACT.Exp).then_inc(expgap_ready, 1)
                for p in range(HEAD_PAIRS[k]):
                    if p > 0:
                        pair(p)
                    if k == 0:
                        if p < 2:
                            w1_high(p + 2)
                        if p < 3:
                            w2_high(p + 1)
                        attn_high(p)
                with act.Fori(HEAD_PAIRS[k], TAIL) as p:
                    pair(p)
                for g in range(TG):
                    pair(TAIL + g, aside=g if k == 0 and g < TG - 1 else None)
                    if k == 0 and g > 0:
                        ln_high(1, g - 1)

            moe(0)
            ln_root(1, TG - 1)

            def u_high(i):
                g, w = divmod(i, 3)
                act.wait_ge(u_done, i + 1)
                act.activation(u[w][:, g * TGW:(g + 1) * TGW], u_bank(i), ACT.Copy).then_inc(uh_ready, 1)

            def u_low(i):
                g, w = divmod(i, 3)
                act.wait_ge(u_rest, i - 5)
                act.activation(u[w][DK:P, g * TGW:(g + 1) * TGW], u_bank(i)[DK:P, :], ACT.Copy).then_inc(ul_act, 1)

            for i in range(9):
                u_high(i)

            def fill(x_, i, f, b):
                kind, n = FILLS[f]
                half = slice(n * TGW, (n + 1) * TGW)
                if kind in "qk":
                    if f == 0:
                        hx = column(act, x_, b)
                        act.activation(hbias[i][:, :], qkbias[:, ds(hx, 1), :].rearrange("p h w -> p (h w)"),
                                       ACT.Copy).then_inc(hbias_ready, 1)
                        act.wait_ge(hbias_ready, x_ + 1)
                    dst, bias = (q1, hbias[i][:, 0:1]) if kind == "q" else (k1, hbias[i][:, 1:2])
                    act.wait_ge(qk_done, 4 * x_ + QK.index(f) + 1)
                    act.activation(dst[i][:, half], extra(f), ACT.Identity, bias=bias).then_inc(qk_hi, 1)
                    if kind == "q":
                        act.activation(q2[i][0:DK, half], extra(f)[0:DK, :], ACT.Identity,
                                       bias=bias[0:DK, :]).then_inc(q2_hi, 1)
                elif kind == "v":
                    act.wait_ge(v_done, x_ + 1)
                    act.activation(vv[i][:, :, 0:DK], extra(f).rearrange("p (j d) -> p j d", d=DK),
                                   ACT.Copy).then_inc(v_hi, 1)
                elif kind == "r":
                    act.wait_ge(maxrows_done, x_ + 1)
                    act.activation(maxrows[i][DK:DK + JB, :], extra(f)[DK:DK + JB, 0:P], ACT.Copy).then_inc(maxrows_ready, 1)

            def copy_acc(h):
                act.wait_ge(pv_done, STEPS * (h + 1))
                wait(act, head_ready, h)
                for b, (lo, hi) in enumerate(((0, 3), (3, 6), (6, 8))):
                    last = act.activation(acc_sb[:, lo:hi, :],
                                          bank[b][:, 0:(hi - lo) * VW].rearrange("p (n c) -> p n c", c=VW),
                                          ACT.Copy)
                last.then_inc(acc_out, 1)

            def head(h, i, b, first=False, last=False):
                for s in range(STEPS):
                    if s == ACC_STEP and not first:
                        copy_acc(h - 1)
                    act.wait_ge(st_done, STEPS * h + s + 1)
                    wait(act, pv_done, STEPS * h + s + 1 - RING)
                    act.activation(prob[s % RING], bank[3 + s % 2][:, :], ACT.Exp, scale=SCALE).then_inc(exp_done, 1)
                    if not last:
                        for f in ACT_FILLS[s]:
                            fill(h + 1, 1 - i, f, b)

            for f in range(len(FILLS)):
                fill(0, 0, f, 0)
                if FILLS[f] == TURN_AFTER:
                    ln_high(1, TG - 1)
                if FILLS[f] in U_AFTER:
                    u_high(9 + U_AFTER.index(FILLS[f]))
                if FILLS[f] in REST_AFTER:
                    u_low(6 + REST_AFTER.index(FILLS[f]))
            run_heads(act, head)
            copy_acc(NH - 1)

            def turned_high(n, i):
                for c in range(2):
                    act.wait_ge(o_turned, 2 * n + c + 1)
                    wait(act, o_done, n - 1)
                    act.activation(oh[i][:, c * TGW:(c + 1) * TGW], bank[2 * i + c][:, :], ACT.Copy).then_inc(oh_ready, 1)

            for p in range(NT // 2):
                for i in range(2):
                    turned_high(2 * p + i, i)
                if p in ROOT_AT:
                    ln_root(2, ROOT_AT.index(p))
                if p in TURN_AT:
                    ln_high(2, TURN_AT.index(p))
            ln_high(2, TG - 2)
            ln_root(2, TG - 1)
            moe(1)

        @block.tensor
        def _(pe):
            def mm3(dst, lh, ll, rh, rl, start=True, stop=True, inc=None):
                pe.matmul(dst, lh, rh, start=start, stop=False, skip_group_check=True)
                pe.matmul(dst, lh, rl, start=False, stop=False, skip_group_check=True)
                last = pe.matmul(dst, ll, rh, start=False, stop=stop, skip_group_check=True)
                if inc is not None:
                    last.then_inc(inc, 1)

            def turn_ln(n, g):
                if n == 0 and g == 0:
                    pe.wait_ge(ident_ready, 1)
                if (n, g) in POOL_NORMS:
                    pe.wait_ge(xn_pool, POOL_NORMS.index((n, g)) + 1)
                else:
                    pe.wait_ge(xn_ready, DVE_NORMS.index((n, g)) + 1)
                if n == 1 and g == 0:
                    pe.wait_ge(b2_added, TG)
                if n == 1 and g == 1:
                    pe.wait_ge(obias_ready, 1)
                if g >= 2:
                    pe.wait_ge(xl_ready, TG * n + g - 1)
                for t in range(TPG):
                    c = (g * TPG + t) * D
                    last = pe.transpose(ln_bank(n, g)[:, t * P:(t + 1) * P], XN[n][:, c:c + D], ident[:, :])
                last.then_inc(xn_turned, 1)

            turn_ln(0, 0)
            pe.wait_ge(rows_in, 16 * 6)
            pe.transpose(bank[5][:, 0:E * FB], rows[:, :], ident[0:E * FB, 0:E * FB])
            pe.transpose(bank[5][:, 96:96 + PAIRS], vrows, ident[0:PAIRS, 0:PAIRS])
            pe.transpose(bank[5][:, 32:32 + H], qkrows[:, 0, :], ident[0:H, 0:H])
            pe.transpose(bank[5][:, 64:64 + H], qkrows[:, 1, :], ident[0:H, 0:H]).then_inc(bias_turned, 1)
            turn_ln(0, 1)

            def moe(k):
                base = k * UNITS

                def logits():
                    if k == 0:
                        pe.wait_ge(gl_ready, 1)
                        pe.wait_ge(bias_ready, 6)
                    pe.wait_ge(xl_ready, TG * (2 * k + 1))
                    for n in range(NT):
                        t = slice(n * P, (n + 1) * P)
                        dst = bank[5][:, n * E:(n + 1) * E]
                        for a, (lhs, rhs) in enumerate(((xh, gh), (xh, gl), (xl, gh), (xl, gl))):
                            last = pe.matmul(dst, lhs[:, t], rhs[:, :], start=(n == 0 and a == 0), stop=(a == 3),
                                             skip_group_check=True)
                    last.then_inc(logit_done, 1)

                def hidden(p, q, e, tg):
                    n = base + 2 * p + q
                    if isinstance(p, int) and p == 0:
                        pe.wait_ge(xl_ready, TG * 2 * k + 1)
                    if k == 0 and isinstance(p, int) and p < 4:
                        pe.wait_ge(w1l_ready, e // 2 + 1)
                    for f in range(FB):
                        wait(pe, gelu_done, FB * (n - 1) + f + 1)
                        c = ds(e * F + f * P, P)
                        t = ds(tg * TGW, TGW)
                        mm3(bank[f][:, :], w1h[:, c], w1l[:, c], xh[:, t], xl[:, t], inc=hid_done)

                def down(p, q, e):
                    n = base + 2 * p + q
                    wait(pe, y_added, n - 1)
                    if isinstance(p, int) and p == 0 and q == 1:
                        pe.wait_ge(logit_read, k + 1)
                    if k == 0 and isinstance(p, int) and p < 4:
                        pe.wait_ge(w2l_ready, e // 2 + 1)
                    for f in range(FB):
                        pe.wait_ge(hl_done, FB * n + f + 1)
                        c = ds((e * FB + f) * D, D)
                        for t in range(TPG):
                            b = slice(t * P, (t + 1) * P)
                            mm3(bank[4 + q][:, b], hh[q][f][:, b], hl[q][f][:, b], w2h[:, c], w2l[:, c],
                                start=(f == 0 and t == 0), stop=(f == FB - 1),
                                inc=y_done if (f, t) == (FB - 1, TPG - 1) else None)

                def at(v):
                    if isinstance(v, int):
                        return v % E, v // E
                    return pe.snap(v % E), pe.snap(v // E)

                def pair(p, last=False, before_first=None, before_down=None):
                    e0, _ = at(2 * p)
                    e1, t1 = at(2 * p + 1)
                    hidden(p, 1, e1, t1)
                    if before_first is not None:
                        before_first()
                    down(p, 0, e0)
                    if not last:
                        e2, t2 = at(2 * p + 2)
                        hidden(p + 1, 0, e2, t2)
                    if before_down is not None:
                        before_down()
                    down(p, 1, e1)

                hidden(0, 0, *at(0))
                for g in LATE[k]:
                    turn_ln(2 * k, g)
                pair(0, before_first=logits)
                for p in range(1, HEAD_PAIRS[k]):
                    pair(p)
                pe.wait_ge(comb_ready, k + 1)
                pe.transpose(bank[6][:, 0:P], comb[:, :, :].rearrange("p n e -> p (n e)"), ident[:, :]).then_inc(comb_turned, 1)
                with pe.Fori(HEAD_PAIRS[k], TAIL) as p:
                    pair(p)
                pe.wait_ge(combT_ready, k + 1)
                pe.wait_ge(b2_in, 16 * NT * (k + 1))
                for g in range(TG):
                    if g >= 1:
                        wait(pe, b2_added, TG * k + g - 1)
                    pe.matmul(bank[6 + (g + 1) % 2][:, :], combT[:, :], b2diag[:, g * TGW:(g + 1) * TGW],
                              start=True, stop=True).then_inc(b2_done, 1)
                for g in range(TG):
                    def between():
                        if k == 0 and g == 0:
                            values_bias()
                        elif k == 0:
                            turn_ln(1, g - 1)
                    pair(TAIL + g, last=g == TG - 1, before_down=between)

            def values_bias():
                pe.wait_ge(al_ready, 4)
                pe.wait_ge(b2_added, TG)
                for c in range(PAIRS):
                    vh, vl = (t[:, c:c + 1].to_broadcast([P, P]) for t in (vbias_h, vbias_l))
                    b = slice(c * D, (c + 1) * D)
                    mm3(bank[7][:, 0:D], vh, vl, fo_h[:, b], fo_l[:, b], start=(c == 0), stop=(c == PAIRS - 1),
                        inc=vbias_done if c == PAIRS - 1 else None)

            moe(0)

            def u_product(i):
                g, w = divmod(i, 3)
                t = slice(g * TGW, (g + 1) * TGW)
                pe.wait_ge(xl_ready, TG + g + 1)
                if i == 0:
                    pe.wait_ge(gelu_done, FB * UNITS)
                if i in (4, 5):
                    pe.wait_ge(y_added, UNITS - 5 + i)
                if i >= 6:
                    pe.wait_ge(ul_ready, min(i - 5, 6))
                if i == 3 * TG - 1:
                    pe.wait_ge(ul_act, 1)
                wh, wl = (m[:, w, :, :].rearrange("p r d -> p (r d)") for m in (pwh, pwl))
                mm3(u_bank(i), wh, wl, xh[:, t], xl[:, t], stop=i < 6, inc=u_done)

            def u_less_high(i):
                g, w = divmod(i, 3)
                pe.wait_ge(uh_ready, i + 1)
                pe.matmul(u_bank(i), minus_ident16[:, :], u[w][:, g * TGW:(g + 1) * TGW], start=False, stop=True,
                          skip_group_check=True).then_inc(u_rest, 1)

            for i in range(9):
                u_product(i)

            def fill(x_, i, f, b):
                kind, n = FILLS[f]
                dst = extra(f)
                g = f - 3 if f >= 3 else max(n for n in range(len(FILLS)) if n % 3 == f)
                y = x_ if f >= 3 else x_ - 1
                pk, pn = FILLS[g]
                if pk in "qk":
                    s, v = qk_lo, 4 * y + QK.index(g) + 1
                elif pk == "v":
                    s, v = v_lo, y + 1
                elif pk == "m":
                    s, v = smax_red, STEPS * y + pn + 1
                else:
                    s, v = maxrows_ready, y + 1
                wait(pe, s, v)
                if kind in "qkv":
                    hx = column(pe, x_, b)
                if kind in "qk":
                    w = "qk".index(kind)
                    uu = u[w][:, b * SEQ + n * TGW:b * SEQ + (n + 1) * TGW]
                    fh, fl = (m[:, w, :, :, :].rearrange("p h r d -> p (h r d)")[:, ds(hx * P, P)]
                              for m in (fqk_h, fqk_l))
                    pe.matmul(dst[:, :], fh, uu, start=True, stop=False)
                    pe.matmul(dst[:, :], fl, uu, start=False, stop=True).then_inc(qk_done, 1)
                elif kind == "v":
                    c = ds(hx * DK, DK)
                    for j in range(JB):
                        uu = u[2][:, b * SEQ + j * P:b * SEQ + (j + 1) * P]
                        pe.matmul(dst[:, j * DK:(j + 1) * DK], uu, fv_h[:, c], start=(j == 0), stop=False,
                                  skip_group_check=True)
                        last = pe.matmul(dst[:, j * DK:(j + 1) * DK], uu, fv_l[:, c], start=False, stop=True,
                                         skip_group_check=True)
                    last.then_inc(v_done, 1)
                elif kind == "m":
                    ib, half = divmod(n, 2)
                    if n < 2:
                        pe.wait_ge(qk_hi, 4 * x_ + 2 * n + 2)
                        pe.wait_ge(qk_lo, 4 * x_ + 1)
                    if n == STEPS // 2:
                        pe.wait_ge(qk_lo, 4 * x_ + 3)
                    pe.matmul(dst[:, :], q1[i][:, ib * P:(ib + 1) * P], k1[i][:, half * TGW:(half + 1) * TGW],
                              start=True, stop=True).then_inc(smax_done, 1)
                else:
                    pe.wait_ge(negmax_ready, x_ + 1)
                    pe.matmul(dst[0:DK + JB, 0:P], negmax[i][:, :], ident16[:, :], start=True,
                              stop=True).then_inc(maxrows_done, 1)

            def scores(h, i, s):
                j, half = divmod(s, 2)
                if s == 0:
                    pe.wait_ge(qk_lo, 4 * h + 4)
                    pe.wait_ge(q2_hi, 2 * h + 2)
                    pe.wait_ge(mrow_ready, h + 1)
                wait(pe, exp_done, STEPS * h + s - 1)
                c, t = slice(j * P, (j + 1) * P), slice(half * TGW, (half + 1) * TGW)
                pe.matmul(bank[3 + s % 2][:, :], k1[i][:, c], q1[i][:, t], start=True, stop=False)
                pe.matmul(bank[3 + s % 2][:, :], k2[i][:, c], q2[i][:, t], start=False, stop=True).then_inc(st_done, 1)

            def values(h, i, s):
                j, half = divmod(s, 2)
                if s == 0:
                    wait(pe, acc_out, h)
                    pe.wait_ge(v_lo, h + 1)
                pe.wait_ge(*split_count(h, s))
                hi = prob[s % RING].bitcast(BF16).rearrange("p (n t) -> p n t", t=2)[:, :, 1]
                for t in range(TPG):
                    blk = half * TPG + t
                    dst = bank[blk // 3][:, blk % 3 * VW:(blk % 3 + 1) * VW]
                    c = slice(t * P, (t + 1) * P)
                    pe.matmul(dst, hi[:, c], vv[i][:, j, 0:VW], start=(j == 0 and blk % 3 == 0), stop=False,
                              skip_group_check=True)
                    last = pe.matmul(dst[:, 0:DK + 1], plow[s % RING][:, c], vv[i][:, j, 0:DK + 1], start=False,
                                     stop=(j == JB - 1), skip_group_check=True)
                last.then_inc(pv_done, 1)

            def head(h, i, b, first=False, last=False):
                for s in range(STEPS):
                    scores(h, i, s)
                    if not last:
                        for f in PE_FILLS[s][0]:
                            fill(h + 1, 1 - i, f, b)
                    for t in PV_AT[s]:
                        if t >= 0:
                            values(h, i, t)
                        elif not first:
                            values(h - 1, 1 - i, t + STEPS)
                    if not last:
                        for f in PE_FILLS[s][1]:
                            fill(h + 1, 1 - i, f, b)

            pe.wait_ge(ul_ready, 6)
            pe.wait_ge(pad_ready, 2)
            pe.wait_ge(xl_ready, 2 * TG - 1)
            for f in range(len(FILLS)):
                fill(0, 0, f, 0)
                if FILLS[f] == TURN_AFTER:
                    turn_ln(1, TG - 1)
                if FILLS[f] in U_AFTER:
                    u_product(9 + U_AFTER.index(FILLS[f]))
                if FILLS[f] in REST_AFTER:
                    u_less_high(6 + REST_AFTER.index(FILLS[f]))
            pe.wait_ge(ul_act, 6)
            run_heads(pe, head)
            for t in range(STEPS - LATE_VALUES, STEPS):
                values(NH - 1, 1, t)

            def turn_heads(n, i):
                wait(pe, ol_ready, 2 * n - 2)
                if n == 0:
                    pe.wait_ge(head_ready, H)
                    pe.wait_ge(acc_out, NH)
                if n == JB:
                    pe.wait_ge(head_ready, NH)
                for c in range(2):
                    for t in range(TPG):
                        src = heads[:, :, :].rearrange("p n d -> p (n d)")[
                            :, ds(n * H * DK + (c * TPG + t) * P, P)]
                        last = pe.transpose(bank[2 * i + c][:, t * P:(t + 1) * P], src, ident[:, :])
                    last.then_inc(o_turned, 1)

            def project(n, i):
                wait(pe, o_added, n - 1)
                pe.wait_ge(ol_ready, 2 * n + 2)
                for c in range(PAIRS):
                    b = slice(c * P, (c + 1) * P)
                    mm3(bank[4 + i][:, 0:D], oh[i][:, b], ol[i][:, b], fo_h[:, b], fo_l[:, b], start=(c == 0),
                        stop=(c == PAIRS - 1), inc=o_done if c == PAIRS - 1 else None)

            def out_pair(p, last=False):
                turn_heads(2 * p + 1, 1)
                project(2 * p, 0)
                if not last:
                    turn_heads(2 * p + 2, 0)
                project(2 * p + 1, 1)

            turn_heads(0, 0)
            for p in range(NT // 2):
                out_pair(p, last=p == NT // 2 - 1)
                if p in TURN_AT:
                    turn_ln(2, TURN_AT.index(p))
            turn_ln(2, TG - 2)
            moe(1)

        @block.vector
        def _(dve):
            steps = [0]

            def then(ins):
                steps[0] += 1
                ins.then_inc(dve_step, 1)
                dve.wait_ge(dve_step, steps[0])

            def tile_stats(t):
                return dve.bn_stats(stats[:, t, :], x[:, t * D:(t + 1) * D])

            def ln_stats(n, g):
                if n == 0:
                    dve.wait_ge(x_in[g], 16)
                for t in range(g * TPG, (g + 1) * TPG):
                    last = tile_stats(t)
                then(last)
                ln_variance(n, g)

            def ln_variance(n, g):
                for t in range(g * TPG, (g + 1) * TPG):
                    last = dve.bn_aggr(mv[:, t, :], stats[:, t, :])
                then(last)
                ts = slice(g * TPG, (g + 1) * TPG)
                dve.tensor_scalar(var_eps[:, ts], mv[:, ts, 1], EPS, None, ALU.add).then_inc(var_ready, 1)

            def ln_rstd(n, g):
                ts = slice(g * TPG, (g + 1) * TPG)
                dve.wait_ge(sd_ready, TG * n + g + 1)
                dve.reciprocal(rstd[:, ts], sd[:, ts]).then_inc(rstd_ready, 1)

            def ln_norm(n, g):
                ln_rstd(n, g)
                dve.wait_ge(rstd_ready, TG * n + g + 1)
                for t in range(g * TPG, (g + 1) * TPG):
                    last = dve.tensor_scalar(XN[n][:, t * D:(t + 1) * D], x[:, t * D:(t + 1) * D], mv[:, t, 0:1],
                                             rstd[:, t:t + 1], ALU.subtract, ALU.mult)
                last.then_inc(xn_ready, 1)

            def ln_low(n, g):
                s = slice(g * TGW, (g + 1) * TGW)
                dve.wait_ge(xh_ready, TG * n + g + 1)
                dve.tensor_tensor(xl[:, s], ln_bank(n, g), xh[:, s], ALU.subtract).then_inc(xl_ready, 1)

            def w2_low(c):
                s = slice(c * 1024, (c + 1) * 1024)
                dve.wait_ge(w2h_ready, c + 1)
                dve.tensor_tensor(w2l[:, s], w2_32[:, s], w2h[:, s], ALU.subtract).then_inc(w2l_ready, 1)

            def attn_low(c):
                dve.wait_ge(ah_ready, c + 1)
                if c == 0:
                    for r in range(2):
                        dve.tensor_tensor(pwl[:, :, r, :], pw32[:, :, :], pwh[:, :, r, :], ALU.subtract)
                    last = dve.tensor_tensor(fv_l[:, :], fv_32, fv_h[:, :], ALU.subtract)
                elif c < 3:
                    for r in range(2):
                        last = dve.tensor_tensor(fqk_l[:, c - 1, :, r, :], fqk_32[:, c - 1, :, :],
                                                 fqk_h[:, c - 1, :, r, :], ALU.subtract)
                else:
                    last = dve.tensor_tensor(fo_l[:, :], fo_32, fo_h[:, :], ALU.subtract)
                last.then_inc(al_ready, 1)

            ln_stats(0, 0)
            ln_norm(0, 0)
            ln_stats(0, 1)
            ln_low(0, 0)
            ln_norm(0, 1)
            dve.wait_ge(gh_ready, 1)
            dve.tensor_tensor(gl[:, :], gate32[:, :], gh[:, :], ALU.subtract).then_inc(gl_ready, 1)
            dve.wait_ge(bias_turned, 1)
            dve.tensor_copy(b1c[:, :], bank[5][:, 0:E * FB]).then_inc(bias_ready, 1)
            dve.tensor_copy(vbias[:, :], bank[5][:, 96:96 + PAIRS]).then_inc(bias_ready, 1)
            dve.tensor_copy(vbias_h[:, :], bank[5][:, 96:96 + PAIRS]).then_inc(bias_ready, 1)
            dve.wait_ge(bias_ready, 3)
            dve.tensor_tensor(vbias_l[:, :], vbias[:, :], vbias_h[:, :], ALU.subtract).then_inc(bias_ready, 1)
            dve.tensor_copy(qkbias[:, :, 0], bank[5][:, 32:32 + H]).then_inc(bias_ready, 1)
            dve.tensor_copy(qkbias[:, :, 1], bank[5][:, 64:64 + H]).then_inc(bias_ready, 1)
            ln_stats(0, 2)
            ln_stats(0, 3)
            ln_low(0, 1)
            ln_norm(0, 2)
            ln_norm(0, 3)

            def router(k):
                dve.wait_ge(logit_done, k + 1)
                dve.tensor_copy(logit[:, :, :].rearrange("p n e -> p (n e)"), bank[5][:, 0:NT * E]).then_inc(logit_read, 1)
                dve.wait_ge(logit_read, k + 1)
                dve.wait_ge(falling_ready, 1)
                order = falling[:, :].unsqueeze(1).to_broadcast([P, NT, E])
                for r, rest in enumerate((logit, masked)):
                    then(dve.tensor_reduce(top[:, r, :], rest[:, :, :], AX.X, ALU.max))
                    then(dve.tensor_tensor(is_top[:, :, :], rest[:, :, :],
                                           top[:, r, :].unsqueeze(2).to_broadcast([P, NT, E]), ALU.is_equal))
                    then(dve.tensor_tensor(is_top[:, :, :], is_top[:, :, :], order, ALU.mult))
                    then(dve.tensor_reduce(first[:, :], is_top[:, :, :], AX.X, ALU.max))
                    then(dve.tensor_tensor(sel[:, r, :, :], is_top[:, :, :],
                                           first[:, :].unsqueeze(2).to_broadcast([P, NT, E]), ALU.is_equal))
                    if r == 0:
                        then(dve.scalar_tensor_tensor(out=masked[:, :, :], in0=sel[:, 0, :, :], scalar=-3.0e38,
                                                      in1=logit[:, :, :], op0=ALU.mult, op1=ALU.add))
                dve.tensor_tensor(gap[:, :], top[:, 1, :], top[:, 0, :], ALU.subtract).then_inc(gap_ready, 1)
                dve.wait_ge(expgap_ready, k + 1)
                then(dve.tensor_scalar(wtop[:, 0, :], expgap[:, :], 1.0, None, ALU.add))
                then(dve.reciprocal(wtop[:, 1, :], wtop[:, 0, :]))
                then(dve.tensor_tensor(wtop[:, 2, :], wtop[:, 1, :], expgap[:, :], ALU.mult))
                for r in range(2):
                    then(dve.tensor_tensor(sel[:, r, :, :], sel[:, r, :, :],
                                           wtop[:, 1 + r, :].unsqueeze(2).to_broadcast([P, NT, E]), ALU.mult))
                then(dve.tensor_tensor(picked[:, :, :], sel[:, 0, :, :], sel[:, 1, :, :], ALU.add))
                dve.tensor_scalar(comb[:, :, :], picked[:, :, :], 0.5, None, ALU.mult).then_inc(comb_ready, 1)
                dve.wait_ge(comb_ready, k + 1)

            def moe(k):
                base = k * UNITS

                def at(v):
                    if isinstance(v, int):
                        return v % E, v // E
                    return dve.snap(v % E), dve.snap(v // E)

                def high(p, q):
                    n = base + 2 * p + q
                    for f in range(FB):
                        dve.wait_ge(gelu_done, FB * n + f + 1)
                        if f == 0:
                            wait(dve, y_done, n - 1)
                        dve.tensor_copy(hh[q][f], g32[q][f]).then_inc(hh_done, 1)

                def add(v, q):
                    e, tg = at(v)
                    dve.wait_ge(y_done, base + v + 1)
                    wait(dve, y_added, base + v)
                    for t in range(TPG):
                        xs = x[:, ds((tg * TPG + t) * D, D)]
                        w = comb[:, :, :].rearrange("p n e -> p (n e)")[:, ds((tg * TPG + t) * E + e, 1)]
                        last = dve.scalar_tensor_tensor(out=xs, in0=bank[4 + q][:, t * P:(t + 1) * P], scalar=w,
                                                        in1=xs, op0=ALU.mult, op1=ALU.add)
                    last.then_inc(y_added, 1)

                def pair(p, aside=(None, None)):
                    high(p, 0)
                    if aside[0] is not None:
                        ln_stats(1, aside[0])
                    add(2 * p - 1, 1)
                    high(p, 1)
                    if aside[1] is not None:
                        ln_norm(1, aside[1])
                    add(2 * p, 0)

                high(0, 0)
                for g in LATE[k]:
                    ln_low(2 * k, g)
                high(0, 1)
                if k == 0:
                    w2_low(0)
                router(k)
                add(0, 0)
                for p in range(HEAD_PAIRS[k]):
                    if p > 0:
                        pair(p)
                    if k == 0:
                        if p < 3:
                            w2_low(p + 1)
                        attn_low(p)
                dve.wait_ge(comb_turned, k + 1)
                dve.tensor_copy(combT[:, :], bank[6][:, 0:P]).then_inc(combT_ready, 1)
                with dve.Fori(HEAD_PAIRS[k], TAIL) as p:
                    pair(p)
                dve.wait_ge(y_added, base + 2 * TAIL - 1)
                for g in range(TG):
                    s = slice(g * TGW, (g + 1) * TGW)
                    dve.wait_ge(b2_done, TG * k + g + 1)
                    last = dve.tensor_tensor(x[:, s], x[:, s], bank[6 + (g + 1) % 2], ALU.add)
                    last.then_inc(b2_added, 1)
                dve.wait_ge(b2_added, TG * (k + 1))
                if k == 0:
                    ln_stats(1, 0)
                for g in range(TG):
                    pair(TAIL + g, aside=((1, 0), (2, 1), (None, 2), (None, None))[g] if k == 0 else (None, None))
                    if k == 0 and g == 0:
                        dve.wait_ge(obias_in, 16)
                        dve.wait_ge(vbias_done, 1)
                        dve.tensor_tensor(obias[:, :], bank[7][:, 0:D], obias[:, :], ALU.add).then_inc(obias_ready, 1)
                    elif k == 0:
                        ln_low(1, g - 1)
                add(UNITS - 1, 1)
                dve.wait_ge(y_added, base + UNITS)

            moe(0)
            ln_stats(1, TG - 1)

            def u_low(i):
                g, w = divmod(i, 3)
                s = slice(g * TGW, (g + 1) * TGW)
                dve.wait_ge(uh_ready, i + 1)
                dve.tensor_tensor(u[w][DK:P, s], u_bank(i)[DK:P, :], u[w][DK:P, s], ALU.subtract).then_inc(ul_ready, 1)

            for i in range(3):
                u_low(i)
            ln_rstd(1, TG - 1)
            for i in range(3, 6):
                u_low(i)

            def fill(x_, i, f, b):
                kind, n = FILLS[f]
                half = slice(n * TGW, (n + 1) * TGW)
                if kind in "qk":
                    dve.wait_ge(qk_hi, 4 * x_ + QK.index(f) + 1)
                    if kind == "q":
                        dve.wait_ge(q2_hi, 2 * x_ + n + 1)
                    if kind == "q":
                        dve.scalar_tensor_tensor(out=q1[i][DK:P, half], in0=extra(f)[DK:P, :],
                                                 scalar=hbias[i][DK:P, 0:1], in1=q1[i][DK:P, half],
                                                 op0=ALU.add, op1=ALU.subtract).then_inc(qk_lo, 1)
                    else:
                        dve.scalar_tensor_tensor(out=k2[i][0:DK, half], in0=extra(f)[0:DK, :],
                                                 scalar=hbias[i][0:DK, 1:2], in1=k1[i][0:DK, half],
                                                 op0=ALU.add, op1=ALU.subtract).then_inc(qk_lo, 1)
                elif kind == "v":
                    dve.wait_ge(v_hi, x_ + 1)
                    dve.tensor_tensor(vv[i][:, :, DK + 1:VW], extra(f).rearrange("p (j d) -> p j d", d=DK),
                                      vv[i][:, :, 0:DK], ALU.subtract).then_inc(v_lo, 1)
                elif kind == "m":
                    dve.wait_ge(smax_done, STEPS * x_ + n + 1)
                    dve.tensor_reduce(tilemax[i][:, n:n + 1], extra(f)[:, :], AX.X, ALU.max).then_inc(smax_red, 1)
                    if n == STEPS - 1:
                        dve.wait_ge(smax_red, STEPS * (x_ + 1))
                        wait(dve, maxrows_done, x_ - 1)
                        dve.tensor_reduce(negmax[i][:, DK:DK + JB], tilemax[i][:, :].rearrange("p (b h) -> p b h", h=2),
                                          AX.X, ALU.max, negate=True).then_inc(negmax_ready, 1)

                elif kind == "r":
                    dve.wait_ge(maxrows_ready, x_ + 1)
                    dve.tensor_tensor(q2[i][DK:DK + JB, :].rearrange("p (t c) -> p t c", c=P),
                                      maxrows[i][DK:DK + JB, :].unsqueeze(1).to_broadcast([JB, JB, P]),
                                      tilemask[DK:DK + JB, :, :], ALU.mult).then_inc(mrow_ready, 1)

            def normalise(h):
                if isinstance(h, int):
                    hx, bx = h % H, h // H
                else:
                    hx, bx = dve.snap(h % H), dve.snap(h // H)
                dve.wait_ge(acc_out, h + 1)
                dve.reciprocal(rsum[:, :], acc_sb[:, :, DK]).then_inc(norm_step, 1)
                dve.wait_ge(norm_step, h + 1)
                dve.wait_ge(acc_sum, h + 1)
                dst = heads[:, ds(bx * JB, JB), ds(hx * DK, DK)]
                dve.tensor_tensor(dst, acc_sb[:, :, 0:DK], rsum[:, :].unsqueeze(2).to_broadcast([P, JB, DK]),
                                  ALU.mult).then_inc(head_ready, 1)

            def head(h, i, b, first=False, last=False):
                for s in range(STEPS):
                    if s == NORM_STEP and not (first or last):
                        normalise(h - 1)
                    if s in dve_splits(last):
                        dve.wait_ge(exp_done, STEPS * h + s + 1)
                        hi = prob[s % RING].bitcast(BF16).rearrange("p (n t) -> p n t", t=2)[:, :, 1]
                        dve.tensor_tensor(plow[s % RING], prob[s % RING], hi, ALU.subtract).then_inc(plow_dve, 1)
                    if not last:
                        for f in DVE_FILLS[s]:
                            fill(h + 1, 1 - i, f, b)

            for f in range(len(FILLS)):
                fill(0, 0, f, 0)
                if FILLS[f] == TURN_AFTER:
                    ln_low(1, TG - 1)
            run_heads(dve, head)
            normalise(NH - 2)
            normalise(NH - 1)

            def turned_low(n, i):
                for c in range(2):
                    b = slice(c * TGW, (c + 1) * TGW)
                    dve.wait_ge(oh_ready, 2 * n + c + 1)
                    dve.tensor_tensor(ol[i][:, b], bank[2 * i + c][:, :], oh[i][:, b], ALU.subtract).then_inc(ol_ready, 1)

            def add_out(n, i):
                dve.wait_ge(o_done, n + 1)
                xs = x[:, ds(n * D, D)]
                dve.tensor_tensor(xs, xs, bank[4 + i][:, 0:D], ALU.add).then_inc(o_added, 1)

            def out_stats(n):
                dve.wait_ge(o_added, n + 1)
                tile_stats(n).then_inc(stats_ready, 1)

            def out_pair(p, first=False):
                turned_low(2 * p, 0)
                if not first:
                    add_out(2 * p - 1, 1)
                    out_stats(2 * p - 2)
                turned_low(2 * p + 1, 1)
                add_out(2 * p, 0)
                if not first:
                    out_stats(2 * p - 1)

            dve.wait_ge(xbias_added, 1)
            for p in range(NT // 2):
                out_pair(p, first=p == 0)
                if p in ROOT_AT:
                    if p < ROOT_AT[-1]:
                        ln_rstd(2, ROOT_AT.index(p))
                    else:
                        ln_norm(2, TG - 2)
                if p in TURN_AT:
                    ln_low(2, TURN_AT.index(p))
                if p in STATS_AT:
                    dve.wait_ge(stats_ready, 2 * p)
                    ln_variance(2, STATS_AT.index(p))
            add_out(NT - 1, 1)
            out_stats(NT - 2)
            out_stats(NT - 1)
            dve.wait_ge(stats_ready, NT)
            ln_variance(2, TG - 1)
            ln_norm(2, TG - 1)
            ln_low(2, TG - 2)
            moe(1)


_INS = ["attn_z", "attn_wq", "attn_wk", "attn_wv", "attn_fcq_w", "attn_fcq_b", "attn_fck_w", "attn_fck_b",
        "attn_fcv_w", "attn_fcv_b", "attn_fco_w", "attn_fco_b", "ffn_gate_w", "ffn_w1", "ffn_b1", "ffn_w2", "ffn_b2"]


def kernel(**inputs):
    import numpy as np
    import concourse.bacc as bacc
    from concourse.bass_utils import run_bass_kernel_spmd

    nc = bacc.Bacc("TRN2", target_bir_lowering=False, num_devices=1)
    arrays, args = {}, []
    for name in _INS:
        a = np.ascontiguousarray(inputs[f"L0_{name}"])
        arrays[name] = a
        args.append(nc.dram_tensor(name, a.shape, mybir.dt.from_np(a.dtype), kind="ExternalInput").ap())
    y = nc.dram_tensor("y", arrays["attn_z"].shape, F32, kind="ExternalOutput").ap()
    macaron_block(nc, *args, y)
    result = run_bass_kernel_spmd(nc, [arrays], core_ids=[0])
    return result.results[0]["y"]
```
